# Optimizing a Trainium2 kernel written in Bass

```python
import numpy as np
import jax
import jax.numpy as jnp

def _softmax(x, axis=-1):
    return jax.nn.softmax(x, axis=axis)

def _gelu(x):
    return jax.nn.gelu(x, approximate=True)

def _silu(x):
    return jax.nn.silu(x)

def _sigmoid(x):
    return jax.nn.sigmoid(x)

def _layernorm(x, axis=-1, eps=1e-05):
    m = jnp.mean(x, axis=axis, keepdims=True)
    v = jnp.var(x, axis=axis, keepdims=True)
    return (x - m) / jnp.sqrt(v + eps)

def _scatter_add(tgt, idx, src, axis=0):
    return tgt.at[idx].add(src)

def _segment_sum(src, seg, n):
    return jax.ops.segment_sum(src, seg, n)
kernel_name = 'mk_prb_d1_jaxref_r4_3783dc'

def setup_inputs(seed: int=0):
    np.random.seed(seed)
    _w = jnp.asarray

    def _L0_attn_setup():
        import jax, jax.numpy as jnp
        import numpy as np
        DIM = 256
        H = 16
        HD = DIM // H
        BS = 64
        SPARSITY = 0.95
        SCALE = HD ** (-0.5)
        key = jax.random.key(seed)
        k1, k2, k3 = jax.random.split(key, 3)
        B, N = (2, 512)
        x = jax.random.normal(k1, (B, N, DIM), jnp.float32)
        qkv_w = jax.random.normal(k2, (3 * DIM, DIM), jnp.float32) * DIM ** (-0.5)
        proj_w = jax.random.normal(k3, (DIM, DIM), jnp.float32) * DIM ** (-0.5)
        proj_b = jnp.zeros((DIM,), jnp.float32)
        return {'x': x, 'qkv_w': qkv_w, 'proj_w': proj_w, 'proj_b': proj_b}
    _L0_attn_in = _L0_attn_setup()

    def _L0_ffn_setup():
        import jax, jax.numpy as jnp
        import numpy as np
        B, S, D = (2, 512, 256)
        E, K, F = (16, 2, 128)
        FS = 256
        key = jax.random.key(seed)
        ks = jax.random.split(key, 8)

        def w(k, shape, fan_in):
            return jax.random.normal(k, shape, jnp.float32) / np.sqrt(fan_in).astype(np.float32)
        return {'x': jax.random.normal(ks[0], (B, S, D), jnp.float32), 'Wr': w(ks[1], (D, E), D), 'Wg': w(ks[2], (E, D, F), D), 'Wu': w(ks[3], (E, D, F), D), 'Wd': w(ks[4], (E, F, D), F), 'Sg': w(ks[5], (D, FS), D), 'Su': w(ks[6], (D, FS), D), 'Sd': w(ks[7], (FS, D), FS)}
    _L0_ffn_in = _L0_ffn_setup()
    _d = {'L0_attn_x': _L0_attn_in['x'], 'L0_attn_qkv_w': _L0_attn_in['qkv_w'], 'L0_attn_proj_w': _L0_attn_in['proj_w'], 'L0_attn_proj_b': _L0_attn_in['proj_b'], 'L0_ffn_Wr': _L0_ffn_in['Wr'], 'L0_ffn_Wg': _L0_ffn_in['Wg'], 'L0_ffn_Wu': _L0_ffn_in['Wu'], 'L0_ffn_Wd': _L0_ffn_in['Wd'], 'L0_ffn_Sg': _L0_ffn_in['Sg'], 'L0_ffn_Su': _L0_ffn_in['Su'], 'L0_ffn_Sd': _L0_ffn_in['Sd']}
    _x0 = _d['L0_attn_x']
    _d['L0_attn_x'] = jax.random.normal(jax.random.fold_in(jax.random.key(seed), 1), (16, 512, 256), dtype=_x0.dtype)
    del _x0
    return _d

def reference(L0_attn_x, L0_attn_qkv_w, L0_attn_proj_w, L0_attn_proj_b, L0_ffn_Wr, L0_ffn_Wg, L0_ffn_Wu, L0_ffn_Wd, L0_ffn_Sg, L0_ffn_Su, L0_ffn_Sd):

    def _L0_attn_ref(x, qkv_w, proj_w, proj_b):
        import jax, jax.numpy as jnp
        import numpy as np
        DIM = 256
        H = 16
        HD = DIM // H
        BS = 64
        SPARSITY = 0.95
        SCALE = HD ** (-0.5)
        B, N, D = x.shape
        qkv = (x @ qkv_w.T).reshape(B, N, 3, H, HD).transpose(2, 0, 3, 1, 4)
        q, k, v = (qkv[0], qkv[1], qkv[2])
        M = N // BS
        qb = q.reshape(B, H, M, BS, HD).mean(axis=3)
        kb = k.reshape(B, H, M, BS, HD).mean(axis=3)
        c = jnp.einsum('bhmd,bhnd->bhmn', qb, kb) * SCALE
        k_keep = max(1, int(round(M * (1.0 - SPARSITY))))
        thresh = jax.lax.top_k(c, k_keep)[0][..., -1:]
        block_mask = (c >= thresh) | jnp.eye(M, dtype=bool)
        tmask = jnp.repeat(jnp.repeat(block_mask, BS, axis=2), BS, axis=3)
        scores = jnp.einsum('bhqd,bhkd->bhqk', q, k) * SCALE
        scores = jnp.where(tmask, scores, -jnp.inf)
        probs = jax.nn.softmax(scores, axis=-1)
        out = jnp.einsum('bhqk,bhkd->bhqd', probs, v)
        out = out.transpose(0, 2, 1, 3).reshape(B, N, D)
        return out @ proj_w.T + proj_b

    def _L0_ffn_ref(x, Wr, Wg, Wu, Wd, Sg, Su, Sd):
        import jax, jax.numpy as jnp
        import numpy as np
        B, S, D = (2, 512, 256)
        E, K, F = (16, 2, 128)
        FS = 256
        b, s, d = x.shape
        T = b * s
        xf = x.reshape(T, d)
        shared = jax.nn.silu(xf @ Sg) * (xf @ Su) @ Sd
        probs = jax.nn.softmax(xf @ Wr, axis=-1)
        topk_p, topk_i = jax.lax.top_k(probs, K)
        n_exp = Wr.shape[1]
        cw = jnp.zeros((T, n_exp), x.dtype).at[jnp.arange(T)[:, None], topk_i].add(topk_p)

        def step(acc, ew):
            wg, wu, wd, c = ew
            y = jax.nn.silu(xf @ wg) * (xf @ wu) @ wd
            return (acc + y * c[:, None], None)
        routed, _ = jax.lax.scan(step, jnp.zeros_like(xf), (Wg, Wu, Wd, cw.T))
        return (routed + shared).reshape(b, s, d)
    x = L0_attn_x
    xn = _layernorm(x, axis=-1)
    x = x + _L0_attn_ref(xn, L0_attn_qkv_w, L0_attn_proj_w, L0_attn_proj_b) + _L0_ffn_ref(xn, L0_ffn_Wr, L0_ffn_Wg, L0_ffn_Wu, L0_ffn_Wd, L0_ffn_Sg, L0_ffn_Su, L0_ffn_Sd)
    return x

_drawn_inputs = setup_inputs


def setup_inputs(seed=0):
    import zlib

    import numpy as np

    out = dict(_drawn_inputs(seed))
    spreads = {'L0_attn_proj_b': (0.0, 0.1)}
    factors = {}
    for name, (base, spread) in spreads.items():
        noise = np.random.default_rng([zlib.crc32(name.encode()), seed]).standard_normal(out[name].shape)
        drawn = base * np.exp(spread * noise) if base else spread * noise
        out[name] = jnp.asarray(drawn.astype(out[name].dtype))
    for name, factor in factors.items():
        out[name] = (out[name] * factor).astype(out[name].dtype)
    return out
```

```python
from contextlib import ExitStack

import concourse.bass as bass
from concourse import mybir

ALU = mybir.AluOpType
ACT = mybir.ActivationFunctionType
AX = mybir.AxisListType.X
F32 = mybir.dt.float32
F32R = mybir.dt.float32r
I32 = mybir.dt.int32

P = 128
MASKED = -float(2 ** 100)
LN_EPS = 1e-5


class Order:

    def __init__(self, engine, sem, base=0):
        self.engine, self.sem, self.base, self.n = engine, sem, base, 0

    def done(self, instruction):
        self.n += 1
        instruction.then_inc(self.sem, 1)

    def wait(self):
        self.engine.wait_ge(self.sem, self.base + self.n)


def f32(ap):
    return ap.bitcast(F32)


class Shapes:

    def __init__(self, x, qkv_wT, Wr, Wg, Sg):
        self.B, self.N, self.D = x.shape
        self.T = self.B * self.N
        self.KD = self.D // P
        self.TB = self.N // P
        self.NT = self.T // P
        self.E, _, self.F = Wg.shape
        self.FS = Sg.shape[1]
        self.H, self.HD = 16, self.D // 16
        self.BS = 64
        self.M = self.N // self.BS
        self.TOPK = 2
        most = (self.TOPK * self.T + self.E * (P - 1)) // P
        self.SLOT_TILES = most + most % 2
        self.GATE_LAG, self.DOWN_LAG = 1, 3


def phase_route(nc, sh, dram, keep):
    B, N, D, KD, TB, NT, E = sh.B, sh.N, sh.D, sh.KD, sh.TB, sh.NT, sh.E
    ST = sh.SLOT_TILES
    with ExitStack() as ctx:
        def sb(name, shape, dt=F32):
            return ctx.enter_context(nc.sbuf_tensor(name, shape, dt))

        def ps(name, shape=(P, 512)):
            return ctx.enter_context(nc.psum_tensor(name, list(shape), F32))

        def sem(name):
            return ctx.enter_context(nc.semaphore(name))

        x_in = [sb(f"x_in{i}", [P, TB, D]) for i in range(2)]
        xn = [sb(f"xn{i}", [P, TB, D]) for i in range(2)]
        bn6 = [sb(f"bn6_{i}", [P, TB, 6]) for i in range(2)]
        mean = [sb(f"mean{i}", [P, TB]) for i in range(2)]
        msum = [sb(f"msum{i}", [P, TB]) for i in range(2)]
        dif = [sb(f"dif{i}", [P, TB]) for i in range(2)]
        dif2 = [sb(f"dif2_{i}", [P, TB]) for i in range(2)]
        m2 = [sb(f"m2_{i}", [P, TB]) for i in range(2)]
        var = [sb(f"var{i}", [P, TB]) for i in range(2)]
        vare = [sb(f"vare{i}", [P, TB]) for i in range(2)]
        rstd = [sb(f"rstd{i}", [P, TB]) for i in range(2)]
        minus_half = sb("minus_half", [P, TB])
        wr = sb("wr", [P, KD, E])
        logitT = [sb(f"logitT{i}", [P, N]) for i in range(2)]
        logit = sb("logit", [P, NT, E])

        CH = NT * E // 512
        by_expert, small, per_tile = [P, NT, E], [P, E], [P, NT]
        route = {name: sb(f"route_{name}", shape) for name, shape in dict(
            top0=per_tile, top1=per_tile, first0=per_tile, first1=per_tile, below2=per_tile, exp2=per_tile,
            sum=per_tile, hot0=by_expert, hot1=by_expert, equal=by_expert, cand=by_expert, rest=by_expert,
            below=by_expert, exps=by_expert, pairs=[P, NT * E], all=[P, NT * E], upto=[P, NT * E],
            ahead=[P, NT * E], ahead2=[P, NT * E], slot_et=[P, NT * E], one=[P, NT * E], count=small,
            tiles=small, end=small, begin=small, base=small, iota_e=small, slot=[P, 2, NT], iota_j=[1, ST],
            expert=[1, ST], pair=[1, ST // 2 + 2 * sh.DOWN_LAG], ended=[1, ST, E]).items()}
        route |= {name: sb(f"route_{name}", shape, I32) for name, shape in dict(
            count_i=small, tiles_i=small, lane=[P, 2, NT], tile=[P, 2, NT], iota_ei=small,
            iota_ji=[1, ST]).items()}
        before = sb("before", [P, P])
        ones = sb("ones", [P, P])
        table_zero = sb("table_zero", [P, ST], I32)

        ps_xT = [[ps(f"ps_xT{i}_{k}") for k in range(KD)] for i in range(2)]
        ps_lT = [ps(f"ps_lT{i}") for i in range(2)]
        ps_l = [ps(f"ps_l{i}") for i in range(2)]

        ps_all, ps_before = ps_xT[0][0:2], ps_xT[1][0:2]
        iota_made = sem("iota_made")
        pairs_ready = sem("pairs_ready")
        below_ready = sem("below_ready")
        exp_ready = sem("exp_ready")
        counts_in_psum = sem("counts_in_psum")
        x_here = [sem(f"x_here{i}") for i in range(2)]
        xn_stored = [sem(f"xn_stored{i}") for i in range(2)]
        table_zeroed = sem("table_zeroed")
        wr_here = sem("wr_here")
        const_made = sem("const_made")
        ident_made = sem("ident_made")
        dve_order = sem("dve_order")
        var_ready = sem("var_ready")
        rstd_ready = sem("rstd_ready")
        xn_ready = sem("xn_ready")
        xT_in_psum = sem("xT_in_psum")
        xT_ready = sem("xT_ready")
        lT_in_psum = sem("lT_in_psum")
        lT_ready = sem("lT_ready")
        l_in_psum = sem("l_in_psum")
        l_ready = sem("l_ready")

        xn_tok = dram["xn"].rearrange("(b t p) d -> b p t d", p=P, t=TB)
        x_tok = dram["x"].rearrange("b (t p) d -> b p t d", p=P)
        one = lambda ap: ap.rearrange("o p t d -> (o p) t d")
        block = ctx.enter_context(nc.Block())
        HB = B // 2

        @block.sync
        def _(sp):
            sp.dma_start(wr[:], dram["Wr"].rearrange("(k p) e -> p k e", p=P)).then_inc(wr_here, 16)
            for i in range(2):
                sp.dma_start(x_in[i][:], one(x_tok[i:i + 1])).then_inc(x_here[i], 16)

            sp.wait_ge(iota_made, 10)
            sp.dma_start(dram["table"].rearrange("(p j) o -> p (j o)", p=P), table_zero[:]).then_inc(table_zeroed, 16)

            def step(b, i, load):
                ready, at, nxt = sp.snap(b + 1), sp.snap(b), sp.snap(b + 2)
                sp.wait_ge(xn_ready, ready)
                sp.dma_start(one(xn_tok[bass.ds(at, 1)]), xn[i][:]).then_inc(xn_stored[i], 16)
                if load:
                    sp.dma_start(x_in[i][:], one(x_tok[bass.ds(nxt, 1)])).then_inc(x_here[i], 16)

            with sp.Fori(0, HB - 1) as h:
                for i in range(2):
                    step(2 * h + i, i, True)
            for i in range(2):
                step(B - 2 + i, i, False)
            for i in range(2):
                sp.wait_ge(xn_stored[i], 16 * HB)
            sp.wait_ge(table_zeroed, 16)

        def route_pairs(order):
            v, r = nc.vector, route

            def do(instruction):
                order.done(instruction)
                order.wait()

            def over_e(ap):
                return ap.unsqueeze(2).broadcast_to([P, NT, E])

            def over_t(ap):
                return ap.unsqueeze(1).broadcast_to([P, NT, E])

            iota_e = over_t(r["iota_e"][:])
            left = logit
            for j in range(2):
                top, first, hot = r[f"top{j}"], r[f"first{j}"], r[f"hot{j}"]
                do(v.tensor_reduce(top[:], left[:], AX, ALU.max))
                do(v.tensor_tensor(r["equal"][:], left[:], over_e(top[:]), ALU.is_equal))
                do(v.scalar_tensor_tensor(out=r["cand"][:], in0=r["equal"][:], scalar=-float(E), in1=iota_e,
                                          op0=ALU.mult, op1=ALU.add))
                do(v.tensor_reduce(first[:], r["cand"][:], AX, ALU.min))
                do(v.tensor_tensor(hot[:], r["cand"][:], over_e(first[:]), ALU.is_equal))
                if j == 0:
                    do(v.scalar_tensor_tensor(out=r["rest"][:], in0=hot[:], scalar=-3e38, in1=logit[:],
                                              op0=ALU.mult, op1=ALU.add))
                    left = r["rest"]
            v.tensor_tensor(r["pairs"][:].rearrange("p (e t) -> p t e", e=E), r["hot0"][:], r["hot1"][:],
                            ALU.add).then_inc(pairs_ready, 1)
            v.tensor_tensor(r["below2"][:], r["top1"][:], r["top0"][:], ALU.subtract)
            v.tensor_tensor(r["below"][:], logit[:], over_e(r["top0"][:]), ALU.subtract).then_inc(below_ready, 1)

            order.engine.wait_ge(counts_in_psum, 1)
            for c in range(CH):
                order.done(v.tensor_copy(r["all"][:, c * 512:(c + 1) * 512], ps_all[c][:]))
            order.wait()
            do(v.tensor_tensor_scan(r["upto"][:], r["one"][:], r["all"][:], 0.0, ALU.mult, ALU.add))
            do(v.tensor_tensor(r["ahead"][:], r["upto"][:], r["all"][:], ALU.subtract))
            upto, ahead = (r[n][:].rearrange("p (e t) -> p e t", e=E) for n in ("upto", "ahead"))
            do(v.tensor_tensor(r["count"][:], upto[:, :, NT - 1], ahead[:, :, 0], ALU.subtract))
            do(v.tensor_scalar(r["count_i"][:], r["count"][:], float(P - 1), None, ALU.add))
            do(v.tensor_scalar(r["tiles_i"][:], r["count_i"][:], 7, None, ALU.logical_shift_right))
            do(v.tensor_copy(r["tiles"][:], r["tiles_i"][:]))
            do(v.tensor_tensor_scan(r["end"][:], r["one"][:, 0:E], r["tiles"][:], 0.0, ALU.mult, ALU.add))
            do(v.tensor_tensor(r["begin"][:], r["end"][:], r["tiles"][:], ALU.subtract))
            do(v.scalar_tensor_tensor(out=r["base"][:], in0=r["begin"][:], scalar=float(P), in1=ahead[:, :, 0],
                                      op0=ALU.mult, op1=ALU.subtract))
            for c in range(CH):
                order.done(v.tensor_tensor(r["ahead2"][:, c * 512:(c + 1) * 512], ps_before[c][:],
                                           r["ahead"][:, c * 512:(c + 1) * 512], ALU.add))
            order.wait()
            do(v.tensor_tensor(r["slot_et"][:].rearrange("p (e t) -> p e t", e=E),
                               r["ahead2"][:].rearrange("p (e t) -> p e t", e=E),
                               r["base"][:].unsqueeze(2).broadcast_to([P, E, NT]), ALU.add))
            slot_te = r["slot_et"][:].rearrange("p (e t) -> p t e", e=E)
            for j in range(2):
                do(v.tensor_tensor(r["cand"][:], slot_te, r[f"hot{j}"][:], ALU.mult))
                do(v.tensor_reduce(r["slot"][:, j, :], r["cand"][:], AX, ALU.add))
            do(v.tensor_copy(keep["slot"][:], r["slot"][:]))
            order.done(v.tensor_scalar(r["lane"][:], keep["slot"][:], P - 1, None, ALU.bitwise_and))
            order.done(v.tensor_scalar(r["tile"][:], keep["slot"][:], 7, None, ALU.logical_shift_right))
            order.wait()
            do(v.scalar_tensor_tensor(out=keep["place"][:], in0=r["lane"][:], scalar=float(ST), in1=r["tile"][:],
                                      op0=ALU.mult, op1=ALU.add))
            do(v.tensor_tensor(r["ended"][:], r["end"][0:1, :].unsqueeze(1).broadcast_to([1, ST, E]),
                               r["iota_j"][:].unsqueeze(2).broadcast_to([1, ST, E]), ALU.is_le))
            do(v.tensor_reduce(r["expert"][:], r["ended"][:], AX, ALU.add))
            do(v.tensor_scalar(r["expert"][:], r["expert"][:], float(E - 1), None, ALU.min))
            by_pair = r["expert"][:].rearrange("o (q u) -> o q u", u=2)
            Q, G, W = ST // 2, sh.GATE_LAG, sh.DOWN_LAG
            do(v.scalar_tensor_tensor(out=r["pair"][:, W:W + Q], in0=by_pair[:, :, 1], scalar=float(E),
                                      in1=by_pair[:, :, 0], op0=ALU.mult, op1=ALU.add))
            do(v.scalar_tensor_tensor(out=keep["experts"][:], in0=r["pair"][:, 0:Q + W], scalar=float(E * E),
                                      in1=r["pair"][:, W - G:W - G + Q + W], op0=ALU.mult, op1=ALU.add))
            order.engine.wait_ge(exp_ready, 1)
            do(v.tensor_reduce(r["sum"][:], r["exps"][:], AX, ALU.add))
            do(v.reciprocal(keep["weight"][:, 0, :], r["sum"][:]))
            do(v.tensor_tensor(keep["weight"][:, 1, :], keep["weight"][:, 0, :], r["exp2"][:], ALU.mult))

        @block.gpsimd
        def _(pool):
            nc.gpsimd.iota(keep["token"][:], pattern=[[P, NT]], base=0, channel_multiplier=1).then_inc(iota_made, 1)
            nc.gpsimd.iota(route["iota_ei"][:], pattern=[[1, E]], base=0, channel_multiplier=0).then_inc(iota_made, 1)
            nc.gpsimd.iota(route["iota_ji"][:], pattern=[[1, ST]], base=0, channel_multiplier=0).then_inc(iota_made, 1)
            nc.gpsimd.memset(route["one"][:], 1.0).then_inc(iota_made, 1)
            nc.gpsimd.memset(route["pair"][:], 0.0).then_inc(iota_made, 1)
            nc.gpsimd.memset(table_zero[:], 0).then_inc(iota_made, 1)
            for i in range(2):
                nc.gpsimd.memset(logitT[i][:], 0.0).then_inc(iota_made, 1)
            pool.wait_ge(iota_made, 8)
            nc.gpsimd.tensor_copy(route["iota_e"][:], route["iota_ei"][:]).then_inc(iota_made, 1)
            nc.gpsimd.tensor_copy(route["iota_j"][:], route["iota_ji"][:]).then_inc(iota_made, 1)
            nc.gpsimd.memset(minus_half[:], -0.5).then_inc(const_made, 1)
            nc.gpsimd.memset(keep["ident"][:], 0.0).then_inc(ident_made, 1)
            nc.gpsimd.memset(before[:], 1.0).then_inc(ident_made, 1)
            nc.gpsimd.memset(ones[:], 1.0).then_inc(ident_made, 1)
            pool.wait_ge(ident_made, 3)
            nc.gpsimd.affine_select(out=keep["ident"][:], in_=keep["ident"][:], compare_op=ALU.not_equal, fill=1.0,
                                    base=0, pattern=[[-1, P]], channel_multiplier=1).then_inc(ident_made, 1)
            nc.gpsimd.affine_select(out=before[:], in_=before[:], compare_op=ALU.is_gt, fill=0.0,
                                    base=0, pattern=[[1, P]], channel_multiplier=-1).then_inc(ident_made, 1)
            pool.wait_ge(const_made, 1)

            def step(b, i):
                pool.wait_ge(var_ready, b + 1)
                nc.gpsimd.tensor_tensor(rstd[i][:], vare[i][:], minus_half[:], ALU.pow).then_inc(rstd_ready, 1)

            with pool.Fori(0, HB) as h:
                for i in range(2):
                    step(2 * h + i, i)

        @block.vector
        def _(dve):
            ORDERED = 4

            def stats(b, h, i):
                order = Order(dve, dve_order, b * ORDERED)
                dve.wait_ge(x_here[i], 16 * h + 16)
                for t in range(TB):
                    last = nc.vector.bn_stats(bn6[i][:, t, :], x_in[i][:, t, :])
                order.done(last)
                order.wait()
                s = bn6[i]
                nc.vector.tensor_tensor(dif[i][:], s[:, :, 1], s[:, :, 4], ALU.subtract)
                nc.vector.tensor_tensor(msum[i][:], s[:, :, 1], s[:, :, 4], ALU.add)
                order.done(nc.vector.tensor_tensor(m2[i][:], s[:, :, 2], s[:, :, 5], ALU.add))
                order.wait()
                nc.vector.tensor_scalar(mean[i][:], msum[i][:], 0.5, None, ALU.mult)
                order.done(nc.vector.tensor_tensor(dif2[i][:], dif[i][:], dif[i][:], ALU.mult))
                order.wait()
                order.done(nc.vector.scalar_tensor_tensor(out=var[i][:], in0=dif2[i][:], scalar=D / 4.0,
                                                          in1=m2[i][:], op0=ALU.mult, op1=ALU.add))
                order.wait()
                nc.vector.tensor_scalar(vare[i][:], var[i][:], 1.0 / D, LN_EPS, ALU.mult, ALU.add).then_inc(var_ready, 1)
                assert order.n == ORDERED

            def norm(b, h, i, first):
                dve.wait_ge(rstd_ready, b + 1)
                if not first:
                    dve.wait_ge(xT_in_psum, b - 1)
                    dve.wait_ge(xn_stored[i], 16 * h)
                for t in range(TB):
                    last = nc.vector.tensor_scalar(xn[i][:, t, :], x_in[i][:, t, :], mean[i][:, t:t + 1],
                                                   rstd[i][:, t:t + 1], ALU.subtract, ALU.mult)
                last.then_inc(xn_ready, 1)

            def take_logits(b, i):
                dve.wait_ge(l_in_psum, b + 1)
                nc.vector.tensor_copy(logit[:, bass.ds(b * TB, TB), :],
                                      ps_l[i][:].rearrange("p (t e) -> p t e", t=TB)[:, :, 0:E]).then_inc(l_ready, 1)

            LAG = 2
            dve.wait_ge(iota_made, 10)
            for b in range(LAG):
                stats(b, b // 2, b % 2)
                norm(b, b // 2, b % 2, True)
            with dve.Fori(1, HB) as h:
                for i in range(2):
                    stats(2 * h + i, h, i)
                    norm(2 * h + i, h, i, False)
                    take_logits(2 * h + i - LAG, i)
            for b in range(B - LAG, B):
                take_logits(b, b % 2)
            dve.wait_ge(l_ready, B)
            route_pairs(Order(dve, dve_order, B * ORDERED))

        @block.tensor
        def _(pe):
            pe.wait_ge(ident_made, 5)
            pe.wait_ge(wr_here, 16)

            def transpose_x(b, i, first):
                pe.wait_ge(xn_ready, b + 1)
                if not first:
                    pe.wait_ge(xT_ready, 2 * b - 2)
                for k in range(KD):
                    for t in range(TB):
                        last = nc.tensor.transpose(ps_xT[i][k][:, t * P:(t + 1) * P],
                                                   xn[i][:, t, k * P:(k + 1) * P], keep["ident"][:])
                last.then_inc(xT_in_psum, 1)

            def router(b, i, first):
                pe.wait_ge(xT_ready, 2 * b + 2)
                if not first:
                    pe.wait_ge(lT_ready, b - 1)
                for k in range(KD):
                    last = nc.tensor.matmul(ps_lT[i][0:E, :], wr[:, k, :], keep["xT"][:, k, bass.ds(b * N, N)],
                                            start=(k == 0), stop=(k == KD - 1))
                last.then_inc(lT_in_psum, 1)

            def logits_by_token(b, i, first):
                pe.wait_ge(lT_ready, b + 1)
                if not first:
                    pe.wait_ge(l_ready, b - 1)
                for t in range(TB):
                    last = nc.tensor.transpose(ps_l[i][:, t * P:(t + 1) * P], logitT[i][:, t * P:(t + 1) * P],
                                               keep["ident"][:])
                last.then_inc(l_in_psum, 1)

            def step(b, i):
                if not (isinstance(b, int) and b < 2):
                    logits_by_token(b - 2, i, isinstance(b, int) and b < 4)
                if not (isinstance(b, int) and b < 1):
                    router(b - 1, 1 - i, isinstance(b, int) and b < 3)
                if not (isinstance(b, int) and b >= B):
                    transpose_x(b, i, isinstance(b, int) and b < 2)

            for b in range(4):
                step(b, b % 2)
            with pe.Fori(2, HB) as h:
                for i in range(2):
                    step(2 * h + i, i)
            logits_by_token(B - 2, 0, False)
            router(B - 1, 1, False)
            logits_by_token(B - 1, 1, False)
            pe.wait_ge(pairs_ready, 1)
            for c in range(CH):
                cols = slice(c * 512, (c + 1) * 512)
                nc.tensor.matmul(ps_before[c][:], before[:], route["pairs"][:, cols], start=True, stop=True)
                last = nc.tensor.matmul(ps_all[c][:], ones[:], route["pairs"][:, cols], start=True, stop=True)
            last.then_inc(counts_in_psum, 1)

        @block.scalar
        def _(act):
            def copy_xT(b, i):
                act.wait_ge(xT_in_psum, b + 1)
                for k in range(KD):
                    nc.scalar.copy(keep["xT"][:, k, bass.ds(b * N, N)], ps_xT[i][k][:]).then_inc(xT_ready, 1)

            def copy_lT(b, i, first):
                act.wait_ge(lT_in_psum, b + 1)
                if not first:
                    act.wait_ge(l_in_psum, b - 1)
                nc.scalar.copy(logitT[i][0:E, :], ps_lT[i][0:E, :]).then_inc(lT_ready, 1)

            copy_xT(0, 0)
            copy_xT(1, 1)
            act.wait_ge(iota_made, 10)
            copy_lT(0, 0, True)
            copy_xT(2, 0)
            copy_lT(1, 1, True)
            copy_xT(3, 1)
            copy_lT(2, 0, False)
            with act.Fori(2, HB) as h:
                for i in range(2):
                    copy_xT(2 * h + i, i)
                    copy_lT(2 * h + i - 1, 1 - i, False)
            copy_lT(B - 1, 1, False)
            act.wait_ge(below_ready, 1)
            nc.scalar.activation(route["exps"][:], route["below"][:], ACT.Exp)
            nc.scalar.activation(route["exp2"][:], route["below2"][:], ACT.Exp).then_inc(exp_ready, 1)


def past(b, n):
    return not isinstance(b, int) or b >= n


def steps(engine, step, total, unroll=2, peeled=None, trailing=0):
    peeled = unroll if peeled is None else peeled
    for b in range(peeled):
        step(b, b % unroll)
    with engine.Fori(peeled // unroll, total // unroll) as h:
        for i in range(unroll):
            step(unroll * h + i, i)
    for b in range(total, total + trailing):
        step(b, b % unroll)


def exact_products(nc, out, lhs, rhs, first=True, last=True):
    todo = [(a[x], b[y]) for a, b in zip(lhs, rhs) for x, y in ((0, 0), (0, 1), (1, 0))]
    for n, (a, b) in enumerate(todo):
        ins = nc.tensor.matmul(out, a, b, start=(first and n == 0), stop=(last and n == len(todo) - 1))
    return ins


def phase_shared(nc, sh, dram, keep):
    B, N, D, KD, TB, NT, FS = sh.B, sh.N, sh.D, sh.KD, sh.TB, sh.NT, sh.FS
    KF = FS // P
    with ExitStack() as ctx:
        def sb(name, shape, dt=F32):
            return ctx.enter_context(nc.sbuf_tensor(name, shape, dt))

        def sem(name):
            return ctx.enter_context(nc.semaphore(name))

        def two(name, shape, dt=F32):
            return [sb(f"{name}{i}", shape, dt) for i in range(2)]

        w_in = sb("sh_w_in", [P, KD, 2, FS])
        wd_in = sb("sh_wd_in", [P, KF, D])
        w_part = [sb(f"sh_w_part{i}", [P, KD, 2, FS], F32R) for i in range(2)]
        wd_part = [sb(f"sh_wd_part{i}", [P, KF, D], F32R) for i in range(2)]
        bias = sb("sh_bias", [P, D])
        xh, xl = two("sh_xh", [P, KD, N], F32R), two("sh_xl", [P, KD, N], F32R)
        x_in = two("sh_x_in", [P, TB, D])
        xb = two("sh_xb", [P, TB, D])
        part = two("sh_part", [P, TB, D])
        th = [sb(f"sh_tanh{f}", [P, N]) for f in range(KF)]
        gs = [sb(f"sh_gs{f}", [P, N]) for f in range(KF)]
        hid = [sb(f"sh_hid{f}", [P, N]) for f in range(KF)]
        hh = [two(f"sh_hh{f}_", [P, N], F32R) for f in range(KF)]
        hl = [two(f"sh_hl{f}_", [P, N], F32R) for f in range(KF)]
        ps_gu = [[ctx.enter_context(nc.psum_tensor(f"sh_ps_gu{f}{g}", [P, N], F32)) for g in range(2)]
                 for f in range(KF)]
        ps_out = [ctx.enter_context(nc.psum_tensor(f"sh_ps_out{i}", [P, 2, D], F32)) for i in range(TB // 2)]

        w_here = sem("sh_w_here")
        w_high = sem("sh_w_high")
        w_low = sem("sh_w_low")
        x_here = [sem(f"sh_x_here{i}") for i in range(2)]
        xT_stored = sem("sh_xT_stored")
        part_stored = [sem(f"sh_part_stored{i}") for i in range(2)]
        xh_ready, xl_ready = sem("sh_xh_ready"), sem("sh_xl_ready")
        gu_in_psum = sem("sh_gu_in_psum")
        tanh_ready = sem("sh_tanh_ready")
        gs_ready = sem("sh_gs_ready")
        hid_ready = sem("sh_hid_ready")
        hh_ready, hl_ready = sem("sh_hh_ready"), sem("sh_hl_ready")
        out_in_psum = sem("sh_out_in_psum")
        xb_ready = sem("sh_xb_ready")
        part_ready = sem("sh_part_ready")
        staged = sem("sh_staged")
        in_table = [sem(f"sh_in_table{i}") for i in range(2)]

        x_tok = dram["x"].rearrange("b (t p) d -> b p t d", p=P)
        part_tok = dram["part"].rearrange("(b t p) d -> b p t d", p=P, t=TB)
        one = lambda ap: ap.rearrange("o p t d -> (o p) t d")
        block = ctx.enter_context(nc.Block())

        @block.sync
        def _(sp):
            for g, w in enumerate((dram["Sg"], dram["Su"])):
                sp.dma_start(w_in[:, :, g, :], w.rearrange("(k p) f -> p k f", p=P)).then_inc(w_here, 16)
            sp.dma_start(wd_in[:], dram["Sd"].rearrange("(k p) d -> p k d", p=P)).then_inc(w_here, 16)
            sp.dma_start(bias[:], dram["proj_b"].broadcast_to([P, D])).then_inc(w_here, 16)
            for i in range(2):
                sp.dma_start(x_in[i][:], one(x_tok[i:i + 1])).then_inc(x_here[i], 16)
            with sp.Fori(0, B) as b:
                at, col = sp.snap(b), sp.snap(b * N)
                sp.dma_start(one(dram["xT"][bass.ds(at, 1)]), keep["xT"][:, :, bass.ds(col, N)]).then_inc(xT_stored, 16)

            def step(b, i):
                ready, at = ((TB // 2) * (b + 1), b) if isinstance(b, int) else (sp.snap((b + 1) * (TB // 2)), sp.snap(b))
                sp.wait_ge(part_ready, ready)
                sp.dma_start(one(part_tok[bass.ds(at, 1)]), part[i][:]).then_inc(part_stored[i], 16)

            def load(b, i):
                used, at = sp.snap(b - 1), sp.snap(b)
                sp.wait_ge(xb_ready, used)
                sp.dma_start(x_in[i][:], one(x_tok[bass.ds(at, 1)])).then_inc(x_here[i], 16)

            with sp.Fori(1, B // 2) as h:
                for i in range(2):
                    load(2 * h + i, i)
                    step(2 * h + i - 2, i)
            for b in range(B - 2, B):
                step(b, b % 2)
            for i in range(2):
                sp.wait_ge(part_stored[i], 16 * (B // 2))
            sp.wait_ge(xT_stored, 16 * B)

        @block.gpsimd
        def _(pool):
            G = 4
            stage_place = [sb(f"sh_stage_place{i}", [P, 2, G], I32) for i in range(2)]
            stage_token = [sb(f"sh_stage_token{i}", [P, G], I32) for i in range(2)]

            def step(h, i):
                if past(h, 2):
                    pool.wait_ge(in_table[i], (h // 2 if isinstance(h, int) else h_half[0]) * (2 * G * 16))
                nc.gpsimd.tensor_copy(stage_place[i][:], keep["place"][:, :, bass.ds(h * G, G)]).then_inc(staged, 1)
                nc.gpsimd.tensor_copy(stage_token[i][:], keep["token"][:, bass.ds(h * G, G)]).then_inc(staged, 1)
                pool.wait_ge(staged, 2)
                pool.sem_clear(staged)
                for t in range(G):
                    for j in range(2):
                        nc.gpsimd.indirect_dma_start(
                            out=dram["table"], out_offset=bass.IndirectOffsetOnAxis(ap=stage_place[i][:, j, t:t + 1], axis=0),
                            in_=stage_token[i][:, t:t + 1], in_offset=None).then_inc(in_table[i], 16)

            S = NT // G
            h_half = [None]
            for h in range(2):
                step(h, h)
            with pool.Fori(1, S // 2) as hh_:
                h_half[0] = hh_
                for i in range(2):
                    step(2 * hh_ + i, i)
            for i in range(2):
                pool.wait_ge(in_table[i], (S // 2) * 2 * G * 16)

        @block.scalar
        def _(act):
            act.wait_ge(w_here, 64)
            nc.scalar.copy(w_part[0][:], w_in[:])
            nc.scalar.copy(wd_part[0][:], wd_in[:]).then_inc(w_high, 1)

            def high_x(b, i):
                if past(b, 2):
                    act.wait_ge(gu_in_psum, KF * b - KF)
                nc.scalar.copy(xh[i][:], keep["xT"][:, :, bass.ds(b * N, N)]).then_inc(xh_ready, 1)

            def tanh(b, f):
                act.wait_ge(gu_in_psum, KF * b + f + 1)
                if past(b, 1):
                    act.wait_ge(gs_ready, KF * b - KF + f + 1)
                nc.scalar.activation(th[f][:], ps_gu[f][0][:], ACT.Tanh, scale=0.5).then_inc(tanh_ready, 1)

            def high_h(b, i, f):
                act.wait_ge(hid_ready, KF * b + f + 1)
                if past(b, 2):
                    act.wait_ge(out_in_psum, (TB // 2) * (b - 1))
                nc.scalar.copy(hh[f][i][:], hid[f][:]).then_inc(hh_ready, 1)

            def step(b, i):
                if not isinstance(b, int) or b < B - 1:
                    high_x(b + 1, 1 - i)
                for f in range(KF):
                    tanh(b, f)
                for f in range(KF):
                    high_h(b, i, f)

            high_x(0, 0)
            step(0, 0)
            step(1, 1)
            with act.Fori(1, B // 2 - 1) as h:
                for i in range(2):
                    step(2 * h + i, i)
            step(B - 2, 0)
            step(B - 1, 1)

        @block.vector
        def _(dve):
            dve.wait_ge(w_high, 1)
            nc.vector.tensor_tensor(w_part[1][:], w_in[:], f32(w_part[0][:]), ALU.subtract)
            nc.vector.tensor_tensor(wd_part[1][:], wd_in[:], f32(wd_part[0][:]), ALU.subtract).then_inc(w_low, 1)

            def low_x(b, i):
                dve.wait_ge(xh_ready, b + 1)
                if past(b, 2):
                    dve.wait_ge(gu_in_psum, KF * b - KF)
                nc.vector.tensor_tensor(xl[i][:], keep["xT"][:, :, bass.ds(b * N, N)], f32(xh[i][:]),
                                        ALU.subtract).then_inc(xl_ready, 1)

            def hidden(b, f):
                dve.wait_ge(tanh_ready, KF * b + f + 1)
                nc.vector.scalar_tensor_tensor(out=gs[f][:], in0=th[f][:], scalar=1.0, in1=ps_gu[f][0][:],
                                               op0=ALU.add, op1=ALU.mult).then_inc(gs_ready, 1)
                dve.wait_ge(gs_ready, KF * b + f + 1)
                if past(b, 1):
                    dve.wait_ge(hh_ready, KF * b - KF + f + 1)
                    dve.wait_ge(hl_ready, KF * b - KF + f + 1)
                nc.vector.scalar_tensor_tensor(out=hid[f][:], in0=gs[f][:], scalar=0.5, in1=ps_gu[f][1][:],
                                               op0=ALU.mult, op1=ALU.mult).then_inc(hid_ready, 1)

            def low_h(b, i, f):
                dve.wait_ge(hh_ready, KF * b + f + 1)
                nc.vector.tensor_tensor(hl[f][i][:], hid[f][:], f32(hh[f][i][:]), ALU.subtract).then_inc(hl_ready, 1)

            def add_bias(b, hb, i):
                dve.wait_ge(x_here[i], 16 * hb + 16)
                nc.vector.tensor_tensor(xb[i][:], x_in[i][:], bias[:].unsqueeze(1).broadcast_to([P, TB, D]),
                                        ALU.add).then_inc(xb_ready, 1)

            def take_out(b, hb, i):
                if past(b, 2):
                    dve.wait_ge(part_stored[i], 16 * hb)
                dve.wait_ge(xb_ready, b + 1)
                for o in range(TB // 2):
                    dve.wait_ge(out_in_psum, (TB // 2) * b + o + 1)
                    nc.vector.tensor_tensor(part[i][:, 2 * o:2 * o + 2, :], ps_out[o][:],
                                            xb[i][:, 2 * o:2 * o + 2, :], ALU.add).then_inc(part_ready, 1)

            def step(b, hb, i, first=False, end=False):
                if not end:
                    low_x(b + 1, 1 - i)
                for f in range(KF):
                    hidden(b, f)
                if not first:
                    take_out(b - 1, hb if i else hb - 1, 1 - i)
                add_bias(b, hb, i)
                for f in range(KF):
                    low_h(b, i, f)

            low_x(0, 0)
            step(0, 0, 0, first=True)
            step(1, 0, 1)
            step(2, 1, 0)
            step(3, 1, 1)
            with dve.Fori(2, B // 2 - 1) as h:
                for i in range(2):
                    step(2 * h + i, h, i)
            step(B - 2, B // 2 - 1, 0)
            step(B - 1, B // 2 - 1, 1, end=True)
            take_out(B - 1, B // 2 - 1, 1)

        @block.tensor
        def _(pe):
            pe.wait_ge(w_low, 1)

            def gate_up(b, i):
                pe.wait_ge(xl_ready, b + 1)
                for f in range(KF):
                    if past(b, 1):
                        pe.wait_ge(hid_ready, KF * b - KF + f + 1)
                    for g in range(2):
                        last = exact_products(
                            nc, ps_gu[f][g][:],
                            [[w_part[x][:, k, g, f * P:(f + 1) * P] for x in range(2)] for k in range(KD)],
                            [[(xh, xl)[x][i][:, k, :] for x in range(2)] for k in range(KD)])
                    last.then_inc(gu_in_psum, 1)

            def down(b, i):
                pe.wait_ge(hl_ready, KF * b + KF)
                for o in range(TB // 2):
                    if past(b, 1):
                        pe.wait_ge(part_ready, (TB // 2) * (b - 1) + o + 1)
                    for t in (2 * o, 2 * o + 1):
                        last = exact_products(
                            nc, ps_out[o][:, t % 2, :],
                            [[(hh, hl)[x][f][i][:, t * P:(t + 1) * P] for x in range(2)] for f in range(KF)],
                            [[wd_part[x][:, f, :] for x in range(2)] for f in range(KF)])
                    last.then_inc(out_in_psum, 1)

            def step(b, i):
                if not (isinstance(b, int) and b >= B):
                    gate_up(b, i)
                if past(b, 1):
                    down(b - 1, 1 - i)

            steps(pe, step, B, peeled=2, trailing=1)


def phase_experts(nc, sh, dram, keep):
    D, KD, E, F, ST = sh.D, sh.KD, sh.E, sh.F, sh.SLOT_TILES
    PAIRS = ST // 2
    U = 4
    WC = 4
    with ExitStack() as ctx:
        def sb(name, shape, dt=F32):
            return ctx.enter_context(nc.sbuf_tensor(f"ex_{name}", shape, dt))

        def ps(name, shape):
            return ctx.enter_context(nc.psum_tensor(f"ex_{name}", shape, F32))

        def sem(name):
            return ctx.enter_context(nc.semaphore(f"ex_{name}"))

        w_in = [sb(f"w_in{i}", [P, WC, KD, 2, F]) for i in range(2)]
        wd_in = [sb(f"wd_in{i}", [P, WC, D]) for i in range(2)]
        w_part = [sb(f"w_part{x}", [P, E, KD, 2 * F], F32R) for x in range(2)]
        wd_part = [sb(f"wd_part{x}", [P, E, D], F32R) for x in range(2)]
        w_rows = [w[:].rearrange("p e k f -> p (e k) f") for w in w_part]
        table = sb("table", [P, ST], I32)
        stage = [sb(f"stage{i}", [P, 2], I32) for i in range(U)]
        xg = [sb(f"xg{i}", [P, 2, D]) for i in range(U)]
        xh = [sb(f"xh{i}", [P, 2 * KD, P], F32R) for i in range(2)]
        xl = [sb(f"xl{i}", [P, 2 * KD, P], F32R) for i in range(2)]
        th = [sb(f"tanh{i}", [P, 2, F]) for i in range(2)]
        gs = [sb(f"gs{i}", [P, 2, F]) for i in range(2)]
        hid = [sb(f"hid{i}", [P, 2, F]) for i in range(2)]
        hh = [sb(f"hh{i}", [P, 2, P], F32R) for i in range(2)]
        hl = [sb(f"hl{i}", [P, 2, P], F32R) for i in range(2)]
        y = [sb(f"y{i}", [P, 2, D]) for i in range(2)]
        ps_x = [ps(f"ps_x{i}", [P, 2 * KD, P]) for i in range(2)]
        ps_gu = [ps(f"ps_gu{i}", [P, 2, 2 * F]) for i in range(2)]
        ps_h = [ps(f"ps_h{i}", [P, 4, P]) for i in range(2)]
        ps_y = [ps(f"ps_y{i}", [P, 2, D]) for i in range(2)]

        w_here = [sem(f"w_here{i}") for i in range(2)]
        w_high, w_low = sem("w_high"), sem("w_low")
        table_here = sem("table_here")
        staged = sem("staged")
        xg_here = [sem(f"xg_here{i}") for i in range(U)]
        x_in_psum, xh_ready, xl_ready = sem("x_in_psum"), sem("xh_ready"), sem("xl_ready")
        gu_in_psum, tanh_ready, gs_ready, hid_ready = (
            sem("gu_in_psum"), sem("tanh_ready"), sem("gs_ready"), sem("hid_ready"))
        h_in_psum, hh_ready, hl_ready = sem("h_in_psum"), sem("hh_ready"), sem("hl_ready")
        y_in_psum, y_ready = sem("y_in_psum"), sem("y_ready")
        y_stored = [sem(f"y_stored{i}") for i in range(2)]
        CHUNKS = E // WC
        block = ctx.enter_context(nc.Block())

        @block.sync
        def _(sp):
            sp.dma_start(table[:], dram["table"].rearrange("(p j) o -> p (j o)", p=P)).then_inc(table_here, 16)
            for c in range(CHUNKS):
                i, experts = c % 2, slice(c * WC, (c + 1) * WC)
                if c >= 2:
                    sp.wait_ge(w_low, c - 1)
                for e in range(WC):
                    for g, w in enumerate((dram["Wg"], dram["Wu"])):
                        sp.dma_start(w_in[i][:, e, :, g, :],
                                     w[c * WC + e].rearrange("(k p) f -> p k f", p=P)).then_inc(w_here[i], 16)
                sp.dma_start(wd_in[i][:], dram["Wd"][experts].rearrange("e f d -> f e d")).then_inc(w_here[i], 16)

            def step(p, i):
                i = i % 2
                at = p * (2 * P) if isinstance(p, int) else sp.snap(p * (2 * P))
                ready = p + 1 if isinstance(p, int) else sp.snap(p + 1)
                sp.wait_ge(y_ready, ready)
                sp.dma_start(dram["y"][bass.ds(at, 2 * P), :].rearrange("(u p) d -> p u d", p=P),
                             y[i][:]).then_inc(y_stored[i], 16)

            steps(sp, step, PAIRS, unroll=2, peeled=0)
            for i in range(2):
                sp.wait_ge(y_stored[i], 16 * (PAIRS // 2))

        @block.gpsimd
        def _(pool):
            pool.wait_ge(table_here, 16)

            def step(p, i):
                if past(p, U):
                    pool.wait_ge(x_in_psum, p - (U - 1))
                nc.gpsimd.tensor_copy(stage[i][:], table[:, bass.ds(2 * p, 2)]).then_inc(staged, 1)
                pool.wait_ge(staged, 1)
                pool.sem_clear(staged)
                for u in range(2):
                    nc.gpsimd.indirect_dma_start(
                        out=xg[i][:, u, :], out_offset=None, in_=dram["xn"],
                        in_offset=bass.IndirectOffsetOnAxis(ap=stage[i][:, u:u + 1], axis=0)).then_inc(xg_here[i], 16)

            steps(pool, step, PAIRS, unroll=U)

        @block.scalar
        def _(act):
            for c in range(CHUNKS):
                i, experts = c % 2, slice(c * WC, (c + 1) * WC)
                act.wait_ge(w_here[i], (2 * WC + 1) * 16 * (c // 2 + 1))
                nc.scalar.copy(w_part[0][:, experts].rearrange("p e k f -> p (e k f)"),
                               w_in[i][:].rearrange("p e k g f -> p (e k g f)"))
                nc.scalar.copy(wd_part[0][:, experts], wd_in[i][:]).then_inc(w_high, 1)

            def step(p, i):
                i = i % 2
                if not (isinstance(p, int) and p >= PAIRS):
                    act.wait_ge(x_in_psum, p + 1)
                    if past(p, 2):
                        act.wait_ge(gu_in_psum, p - 1)
                    nc.scalar.copy(xh[i][:], ps_x[i][:]).then_inc(xh_ready, 1)
                if past(p, 1) and not (isinstance(p, int) and p - 1 >= PAIRS):
                    act.wait_ge(gu_in_psum, p)
                    if past(p, 3):
                        act.wait_ge(gs_ready, p - 2)
                    nc.scalar.activation(th[1 - i][:], ps_gu[1 - i][:, :, 0:F], ACT.Tanh, scale=0.5).then_inc(tanh_ready, 1)
                if past(p, 2) and not (isinstance(p, int) and p - 2 >= PAIRS):
                    act.wait_ge(h_in_psum, p - 1)
                    if past(p, 4):
                        act.wait_ge(y_in_psum, p - 3)
                    nc.scalar.copy(hh[i][:], ps_h[i][:, 0:2, :]).then_inc(hh_ready, 1)
                if past(p, 3):
                    act.wait_ge(y_in_psum, p - 2)
                    if past(p, 5):
                        act.wait_ge(y_stored[1 - i], stored(p))
                    nc.scalar.copy(y[1 - i][:], ps_y[1 - i][:]).then_inc(y_ready, 1)

            half = [None]

            def stored(p):
                if isinstance(p, int):
                    return 16 * ((p - 3) // 2)
                h, i = half[0]
                return (2 * h + (i - 3) // 2) * 16

            for p in range(8):
                step(p, p % 4)
            with act.Fori(2, PAIRS // 4) as h:
                for i in range(4):
                    half[0] = (h, i)
                    step(4 * h + i, i)
            for p in range(PAIRS, PAIRS + 3):
                step(p, p % 4)

        @block.vector
        def _(dve):
            for c in range(CHUNKS):
                i, experts = c % 2, slice(c * WC, (c + 1) * WC)
                dve.wait_ge(w_high, c + 1)
                nc.vector.tensor_tensor(w_part[1][:, experts].rearrange("p e k f -> p (e k f)"),
                                        w_in[i][:].rearrange("p e k g f -> p (e k g f)"),
                                        f32(w_part[0][:, experts]).rearrange("p e k f -> p (e k f)"), ALU.subtract)
                nc.vector.tensor_tensor(wd_part[1][:, experts], wd_in[i][:], f32(wd_part[0][:, experts]),
                                        ALU.subtract).then_inc(w_low, 1)

            def step(p, i):
                i = i % 2
                if not (isinstance(p, int) and p >= PAIRS):
                    dve.wait_ge(xh_ready, p + 1)
                    nc.vector.tensor_tensor(xl[i][:], ps_x[i][:], f32(xh[i][:]), ALU.subtract).then_inc(xl_ready, 1)
                if past(p, 1) and not (isinstance(p, int) and p - 1 >= PAIRS):
                    dve.wait_ge(tanh_ready, p)
                    nc.vector.scalar_tensor_tensor(out=gs[1 - i][:], in0=th[1 - i][:], scalar=1.0,
                                                   in1=ps_gu[1 - i][:, :, 0:F], op0=ALU.add, op1=ALU.mult).then_inc(gs_ready, 1)
                if past(p, 2) and not (isinstance(p, int) and p - 2 >= PAIRS):
                    dve.wait_ge(hh_ready, p - 1)
                    nc.vector.tensor_tensor(hl[i][:], ps_h[i][:, 0:2, :], f32(hh[i][:]), ALU.subtract).then_inc(hl_ready, 1)
                if past(p, 1) and not (isinstance(p, int) and p - 1 >= PAIRS):
                    dve.wait_ge(gs_ready, p)
                    if past(p, 3):
                        dve.wait_ge(h_in_psum, p - 2)
                    nc.vector.scalar_tensor_tensor(out=hid[1 - i][:], in0=gs[1 - i][:], scalar=0.5,
                                                   in1=ps_gu[1 - i][:, :, F:2 * F], op0=ALU.mult, op1=ALU.mult).then_inc(hid_ready, 1)

            steps(dve, step, PAIRS, unroll=4, peeled=4, trailing=2)

        @block.tensor
        def _(pe):
            def experts_of(p):
                word = pe.value_load(keep["experts"][0:1, bass.ds(p, 1)], min_val=0, max_val=E ** 4 - 1)
                return [pe.snap((word // E ** n) % E, min_val=0, max_val=E - 1) for n in range(4)]

            def transpose_x(p, i):
                pe.wait_ge(xg_here[i], gathered(p))
                if past(p, 2):
                    pe.wait_ge(xl_ready, p - 1)
                for u in range(2):
                    for k in range(KD):
                        last = nc.tensor.transpose(ps_x[i % 2][:, u * KD + k, :], xg[i][:, u, k * P:(k + 1) * P],
                                                   keep["ident"][:])
                last.then_inc(x_in_psum, 1)

            def gate_up(p, i, experts):
                pe.wait_ge(xl_ready, p + 1)
                if past(p, 2):
                    pe.wait_ge(hid_ready, p - 1)
                for u in range(2):
                    e = experts[u]
                    last = exact_products(
                        nc, ps_gu[i][:, u, :],
                        [[(xh, xl)[x][i][:, u * KD + k, :] for x in range(2)] for k in range(KD)],
                        [[w_rows[x][:, bass.ds(e * KD + k, 1), :] for x in range(2)] for k in range(KD)])
                last.then_inc(gu_in_psum, 1)

            def transpose_h(p, i):
                pe.wait_ge(hid_ready, p + 1)
                if past(p, 2):
                    pe.wait_ge(hl_ready, p - 1)
                for u in range(2):
                    last = nc.tensor.transpose(ps_h[i][:, u, :], hid[i][:, u, :], keep["ident"][:])
                last.then_inc(h_in_psum, 1)

            def down(p, i, experts):
                pe.wait_ge(hl_ready, p + 1)
                if past(p, 2):
                    pe.wait_ge(y_ready, p - 1)
                for u in range(2):
                    e = experts[u]
                    last = exact_products(nc, ps_y[i][:, u, :], [[(hh, hl)[x][i][:, u, :] for x in range(2)]],
                                          [[wd_part[x][:, bass.ds(e, 1), :] for x in range(2)]])
                last.then_inc(y_in_psum, 1)

            group = [None]

            def gathered(p):
                return 32 * (p // U + 1) if isinstance(p, int) else 32 * group[0] + 32

            def step(p, i):
                inside = not isinstance(p, int) or p < PAIRS
                experts = experts_of(p)
                if inside:
                    transpose_x(p, i)
                i = i % 2
                if past(p, 1) and not (isinstance(p, int) and p - 1 >= PAIRS):
                    gate_up(p - 1, 1 - i, experts[0:2])
                if past(p, 2) and not (isinstance(p, int) and p - 2 >= PAIRS):
                    transpose_h(p - 2, i)
                if past(p, 3):
                    down(p - 3, 1 - i, experts[2:4])

            for p in range(U):
                if p == 1:
                    pe.wait_ge(w_low, CHUNKS)
                step(p, p)
            with pe.Fori(1, PAIRS // U) as h:
                group[0] = h
                for i in range(U):
                    step(U * h + i, i)
            for p in range(PAIRS, PAIRS + 3):
                step(p, p % U)


def phase_attention(nc, sh, dram, keep):
    B, N, D, KD, TB, H, HD, M, BS = sh.B, sh.N, sh.D, sh.KD, sh.TB, sh.H, sh.HD, sh.M, sh.BS
    G = 4
    Q = H // G
    HG = P // HD
    QK0 = M
    TOP0 = M + 4 * HD
    ROWS = TOP0 + 2
    PARTS = ((0, 1, 0, 1), (0, 1, 1, 0))
    with ExitStack() as ctx:
        def sb(name, shape, dt=F32):
            return ctx.enter_context(nc.sbuf_tensor(f"at_{name}", shape, dt))

        def ps(name, shape):
            return ctx.enter_context(nc.psum_tensor(f"at_{name}", shape, F32))

        def sem(name):
            return ctx.enter_context(nc.semaphore(f"at_{name}"))

        stack = [[sb(f"stack{s}{q}", [ROWS, G, N], F32R) for q in range(Q)] for s in range(2)]
        pt = [sb(f"pt{i}", [P, G, TB, N]) for i in range(2)]
        w_part = [sb(f"w_part{x}", [P, KD, 3 * D], F32R) for x in range(2)]
        wp_part = [sb(f"wp_part{x}", [P, KD, D], F32R) for x in range(2)]
        w_in = pt[0][:].rearrange("p g t n -> p (g t n)")[:, 0:KD * 3 * D].rearrange("p (k d) -> p k d", k=KD)
        wp_in = pt[1][:].rearrange("p g t n -> p (g t n)")[:, 0:KD * D].rearrange("p (k d) -> p k d", k=KD)
        vx = sb("vx", [P, TB, H, 2 * HD])
        x_in = sb("x_in", [P, KD, N])
        xh, xl = sb("xh", [P, KD, N], F32R), sb("xl", [P, KD, N], F32R)
        qk_part = [[sb(f"qk_part{s}{x}", [P, N], F32R) for x in range(2)] for s in range(2)]
        qk_sum = [[sb(f"qk_sum{s}{g}", [P, M]) for g in range(KD)] for s in range(2)]
        own_head = sb("own_head", [P, HG])
        k_own = sb("k_own", [P, HG, M])
        c_top = sb("c_top", [M, HG])
        kept = sb("kept", [M, HG, M])
        kept2 = sb("kept2", [M, HG, M])
        eye = sb("eye", [M, M])
        mask = [sb(f"mask{g}", [M, HG, M]) for g in range(KD)]
        top = [sb(f"top{i}", [P, G * TB]) for i in range(2)]
        top_part = [[sb(f"top_part{i}{x}", [G * TB, P], F32R) for x in range(2)] for i in range(2)]
        o_unit = sb("o_unit", [P, N])
        rec = sb("rec", [P, TB, G])
        on = sb("on", [P, TB, D])
        on_part = [sb(f"on_part{x}", [P, KD, N], F32R) for x in range(2)]
        part = sb("part", [P, TB, D])
        yg = [sb(f"yg{j}", [P, TB, D]) for j in range(2)]
        stage = sb("stage", [P, 2, TB], I32)
        ps_s = [ps(f"ps_s{i}", [P, N]) for i in range(2)]
        ps_st = [ps(f"ps_st{i}", [P, 2, N]) for i in range(2)]
        ps_pv = ps("ps_pv", [P, N])
        ps_m = ps("ps_m", [P, TB, P])

        w_here, w_high, w_low = sem("w_here"), sem("w_high"), sem("w_low")
        consts, consts2, const_rows = sem("consts"), sem("consts2"), sem("const_rows")
        x_here, xh_ready, xl_ready = sem("x_here"), sem("xh_ready"), sem("xl_ready")
        qk_in_psum, qk_high, qk_low, qk_taken = sem("qk_in_psum"), sem("qk_high"), sem("qk_low"), sem("qk_taken")
        qk_out = [sem(f"qk_out{g}") for g in range(KD)]
        k_own_ready, c_in_psum, select_order, mask_ready = (
            sem("k_own_ready"), sem("c_in_psum"), sem("select_order"), sem("mask_ready"))
        stack_here = [sem(f"stack_here{q}") for q in range(Q)]
        mask_rows = sem("mask_rows")
        s_in_psum, s_max = sem("s_in_psum"), sem("s_max")
        top_in_psum, top_high, top_low = sem("top_in_psum"), sem("top_high"), sem("top_low")
        top_here = [sem(f"top_here{i}") for i in range(2)]
        st_in_psum, exp_ready = sem("st_in_psum"), sem("exp_ready")
        v_in_psum, v_ready = sem("v_in_psum"), sem("v_ready")
        pv_in_psum, pv_ready = sem("pv_in_psum"), sem("pv_ready")
        ot_in_psum, rec_ready, on_ready = sem("ot_in_psum"), sem("rec_ready"), sem("on_ready")
        on_in_psum, on_high, on_low = sem("on_in_psum"), sem("on_high"), sem("on_low")
        fin_in_psum, fin_ready = sem("fin_in_psum"), sem("fin_ready")
        staged, y_here, added = sem("staged"), sem("y_here"), sem("added")
        part_here, out_stored = sem("part_here"), sem("out_stored")

        tokens = lambda t: t.rearrange("(b t p) d -> b p t d", p=P, t=TB)
        part_tok = tokens(dram["part"])
        out_tok = dram["out"].rearrange("b (t p) d -> b p t d", p=P)
        one = lambda ap: ap.rearrange("o p t d -> (o p) t d")
        block = ctx.enter_context(nc.Block())

        def batches(engine, body):
            body(0, first=True)
            with engine.Fori(1, B - 1) as b:
                body(b)
            body(B - 1, last=True)

        @block.sync
        def _(sp):
            sp.dma_start(w_in, dram["qkv_wT"].rearrange("(k p) d -> p k d", p=P)).then_inc(w_here, 16)
            sp.dma_start(wp_in, dram["proj_wT"].rearrange("(k p) d -> p k d", p=P)).then_inc(w_here, 16)

            def val(x):
                return x if isinstance(x, int) else sp.snap(x)

            def load_x(b):
                at, used = val(b), (b if isinstance(b, int) else sp.snap(b))
                if past(b, 1):
                    sp.wait_ge(xl_ready, used)
                sp.dma_start(x_in[:], one(dram["xT"][bass.ds(at, 1)])).then_inc(x_here, 16)

            def store_qk(b, g):
                at = val(b)
                for s in range(2):
                    ready = val(2 * KD * b + 2 * g + s + 1)
                    sp.wait_ge(qk_taken, ready)
                    for x in range(2):
                        sp.dma_start(dram["qkT"][bass.ds(at, 1), s, g, x].rearrange("o p n -> (o p) n"),
                                     f32(qk_part[s][x][:])).then_inc(qk_out[g], 16)

            def load_stack(b, q):
                at, out = val(b), val(64 * b + 64)
                sp.wait_ge(qk_out[q // 2], out)
                lanes = slice((q % 2) * G * HD, (q % 2 + 1) * G * HD)
                for s in range(2):
                    for r, x in enumerate(PARTS[s]):
                        row = QK0 + r * HD
                        src = dram["qkT"][bass.ds(at, 1), s, q // 2, x, lanes, :]
                        sp.dma_start(f32(stack[s][q][row:row + HD, :, :]),
                                     src.rearrange("o (h d) n -> (o d) h n", d=HD)).then_inc(stack_here[q], 16)

            def top_rows(b, q):
                ready = val(Q * b + q + 1)
                sp.wait_ge(top_low, ready)
                for x in range(2):
                    sp.dma_start(f32(stack[0][q][TOP0 + x:TOP0 + x + 1, :, :]).rearrange("o g n -> o (g n)"),
                                 f32(top_part[q % 2][x][:])).then_inc(top_here[q % 2], 16)

            def store_out(b):
                at, ready = val(b), val(2 * b + 2)
                sp.wait_ge(fin_ready, ready)
                sp.dma_start(one(out_tok[bass.ds(at, 1)]), part[:]).then_inc(out_stored, 16)

            def load_part(b):
                at, stored = val(b), val(16 * b)
                if past(b, 1):
                    sp.wait_ge(out_stored, stored)
                sp.dma_start(part[:], one(part_tok[bass.ds(at, 1)])).then_inc(part_here, 16)

            load_x(0)
            sp.wait_ge(consts, 1)
            for q in range(Q):
                sp.dma_start(f32(stack[1][q][TOP0:ROWS, :, :]),
                             part[0:2, 0:2, :].rearrange("p t d -> p (t d)").unsqueeze(1)
                             .broadcast_to([2, G, N])).then_inc(const_rows, 16)
            for g in range(KD):
                store_qk(0, g)
            for q in range(Q):
                load_stack(0, q)
            sp.wait_ge(const_rows, 16 * Q)
            load_part(0)
            top_rows(0, 0)

            def body(b, first=False, last=False):
                if not last:
                    load_x(b + 1)
                top_rows(b, 1)
                if not first:
                    load_stack(b, 3)
                top_rows(b, 2)
                if not last:
                    store_qk(b + 1, 0)
                    load_stack(b + 1, 0)
                    load_stack(b + 1, 1)
                    store_qk(b + 1, 1)
                if not first:
                    store_out(b - 1)
                top_rows(b, 3)
                if not last:
                    top_rows(b + 1, 0)
                    load_stack(b + 1, 2)
                if not first:
                    load_part(b)

            batches(sp, body)
            store_out(B - 1)
            sp.wait_ge(out_stored, 16 * B)

        @block.gpsimd
        def _(pool):
            nc.gpsimd.memset(part[0:2, 0:2, :], -1.0).then_inc(consts, 1)
            nc.gpsimd.memset(vx[:], 0.0).then_inc(consts2, 1)
            for t in (o_unit[0:M, :], eye[:], own_head[:]):
                nc.gpsimd.memset(t, 1.0).then_inc(consts2, 1)
            pool.wait_ge(consts2, 4)
            nc.gpsimd.memset(vx[:, :, :, HD:HD + 1], 1.0).then_inc(consts2, 1)
            for sign, lanes, t, pattern in ((1, M, o_unit[0:M, :], [[1, M], [0, BS]]), (1, M, eye[:], [[1, M]])):
                nc.gpsimd.affine_select(out=t, in_=t, compare_op=ALU.is_equal, fill=0.0, base=0, pattern=pattern,
                                        channel_multiplier=-1).then_inc(consts2, 1)
            nc.gpsimd.affine_select(out=own_head[:], in_=own_head[:], compare_op=ALU.is_ge, fill=0.0, base=0,
                                    pattern=[[-HD, HG]], channel_multiplier=1).then_inc(consts2, 1)
            pool.wait_ge(consts2, 8)
            nc.gpsimd.affine_select(out=own_head[:], in_=own_head[:], compare_op=ALU.is_gt, fill=0.0, base=HD,
                                    pattern=[[HD, HG]], channel_multiplier=-1).then_inc(consts2, 1)

            def low_x(b):
                pool.wait_ge(xh_ready, b + 1)
                nc.gpsimd.tensor_tensor(xl[:], x_in[:], f32(xh[:]), ALU.subtract).then_inc(xl_ready, 1)

            def mask_quad(b, q, first=False):
                pool.wait_ge(mask_ready, KD * b + q // 2 + 1)
                if not first:
                    pool.wait_ge(st_in_psum, 2 * G * (Q * (b - 1) + q + 1))
                heads = mask[q // 2][:, (q % 2) * G:(q % 2 + 1) * G, :].rearrange("m h n -> m (h n)")
                heads = heads.unsqueeze(2).broadcast_to([M, G * M, BS])
                nc.gpsimd.tensor_tensor(stack[1][q][0:M, :, :].rearrange("m h (n c) -> m (h n) c", c=BS),
                                        heads, heads, ALU.add).then_inc(mask_rows, 1)

            def gather_y(b):
                if past(b, 1):
                    pool.wait_ge(added, 2 * TB * b)
                nc.gpsimd.tensor_copy(stage[:], keep["slot"][:, :, bass.ds(TB * b, TB)]).then_inc(staged, 1)
                pool.wait_ge(staged, 1)
                pool.sem_clear(staged)
                for j in range(2):
                    for t in range(TB):
                        nc.gpsimd.indirect_dma_start(
                            out=yg[j][:, t, :], out_offset=None, in_=dram["y"],
                            in_offset=bass.IndirectOffsetOnAxis(ap=stage[:, j, t:t + 1], axis=0)).then_inc(y_here, 16)

            low_x(0)
            for q in range(Q):
                mask_quad(0, q, first=True)

            def body(b, first=False, last=False):
                if not last:
                    low_x(b + 1)
                    for q in (0, 1):
                        mask_quad(b + 1, q)
                gather_y(b)
                if not last:
                    for q in (2, 3):
                        mask_quad(b + 1, q)

            batches(pool, body)

        @block.scalar
        def _(act):
            act.wait_ge(w_here, 32)
            nc.scalar.copy(w_part[0][:], w_in)
            nc.scalar.copy(wp_part[0][:], wp_in).then_inc(w_high, 1)
            act.wait_ge(consts2, 9)
            for q in range(Q):
                last = nc.scalar.copy(stack[0][q][0:M, :, :], o_unit[0:M, :].unsqueeze(1).broadcast_to([M, G, N]))
            last.then_inc(consts, 1)

            def high_x(b):
                act.wait_ge(x_here, 16 * b + 16)
                if past(b, 1):
                    act.wait_ge(v_in_psum, 2 * b)
                nc.scalar.copy(xh[:], x_in[:]).then_inc(xh_ready, 1)

            def high_qk(b, j):
                g, s = j // 2, j % 2
                act.wait_ge(qk_in_psum, 2 * KD * b + j + 1)
                if g == 1:
                    act.wait_ge(qk_out[0], 64 * b + 64)
                elif past(b, 1):
                    act.wait_ge(qk_out[1], 64 * b)
                nc.scalar.copy(qk_part[s][0][:], ps_s[s][:]).then_inc(qk_high, 1)

            def take_v(b):
                for o in range(2):
                    act.wait_ge(v_in_psum, 2 * b + o + 1)
                    if past(b, 1):
                        act.wait_ge(pv_in_psum, Q * b)
                    nc.scalar.copy(vx[:, 2 * o:2 * o + 2, :, 0:HD],
                                   ps_s[o][:].rearrange("p (t h d) -> p t h d", t=2, h=H)).then_inc(v_ready, 1)

            def take_pv(u):
                act.wait_ge(pv_in_psum, u + 1)
                if past(u, 1):
                    act.wait_ge(ot_in_psum, u)
                nc.scalar.copy(o_unit[:], ps_pv[:]).then_inc(pv_ready, 1)

            def exps(u, i, g):
                for half in range(2):
                    act.wait_ge(st_in_psum, 2 * G * u + 2 * g + half + 1)
                    if past(u, 2) and g == 0 and half == 0:
                        act.wait_ge(pv_in_psum, u - 1)
                    nc.scalar.activation(pt[i][:, g, 2 * half:2 * half + 2, :], ps_st[half][:], ACT.Exp,
                                         scale=float(HD) ** -0.5).then_inc(exp_ready, 1)

            def high_on(b):
                for c in range(KD):
                    act.wait_ge(on_in_psum, KD * b + c + 1)
                    if past(b, 1):
                        act.wait_ge(fin_in_psum, 2 * b)
                    nc.scalar.copy(on_part[0][:, c, :], ps_s[c][:]).then_inc(on_high, 1)

            def stage_of(b, q):
                u = Q * b + q
                if past(u, 2) and (past(b, 1) or q >= 2):
                    take_pv(u - 2)
                for g in range(G):
                    exps(u, q % 2, g)

            high_x(0)
            for j in range(2 * KD):
                high_qk(0, j)

            def body(b, first=False, last=False):
                stage_of(b, 0)
                take_v(b)
                if not last:
                    high_x(b + 1)
                stage_of(b, 1)
                if not last:
                    for j in range(2 * KD):
                        high_qk(b + 1, j)
                if not first:
                    high_on(b - 1)
                stage_of(b, 2)
                stage_of(b, 3)

            batches(act, body)
            take_pv(Q * B - 2)
            take_pv(Q * B - 1)
            high_on(B - 1)

        @block.vector
        def _(dve):
            v = nc.vector
            dve.wait_ge(w_high, 1)
            v.tensor_tensor(w_part[1][:], w_in, f32(w_part[0][:]), ALU.subtract)
            v.tensor_tensor(wp_part[1][:], wp_in, f32(wp_part[0][:]), ALU.subtract).then_inc(w_low, 1)
            dve.wait_ge(consts2, 9)

            def take_qk(b, j):
                g, s = j // 2, j % 2
                dve.wait_ge(qk_high, 2 * KD * b + j + 1)
                v.tensor_tensor(qk_part[s][1][:], ps_s[s][:], f32(qk_part[s][0][:]), ALU.subtract).then_inc(qk_low, 1)
                v.tensor_reduce(qk_sum[s][g][:], ps_s[s][:].rearrange("p (m c) -> p m c", c=BS), AX,
                                ALU.add).then_inc(qk_taken, 1)

            def own_k(b, g):
                dve.wait_ge(qk_taken, 2 * KD * b + 2 * g + 2)
                if g == 1:
                    dve.wait_ge(c_in_psum, KD * b + 1)
                elif past(b, 1):
                    dve.wait_ge(c_in_psum, KD * b)
                v.tensor_tensor(k_own[:], qk_sum[1][g][:].unsqueeze(1).broadcast_to([P, HG, M]),
                                own_head[:].unsqueeze(2).broadcast_to([P, HG, M]), ALU.mult).then_inc(k_own_ready, 1)

            def select(b, g):
                order = Order(dve, select_order, 3 * (KD * b + g))
                dve.wait_ge(c_in_psum, KD * b + g + 1)
                c = ps_m[0:M, 0, 0:HG * M].rearrange("m (h n) -> m h n", h=HG)
                order.done(v.tensor_reduce(c_top[:], c, AX, ALU.max))
                order.wait()
                order.done(v.tensor_tensor(kept[:], c, c_top[:].unsqueeze(2).broadcast_to([M, HG, M]), ALU.is_ge))
                order.wait()
                order.done(v.tensor_tensor(kept2[:], kept[:], eye[:].unsqueeze(1).broadcast_to([M, HG, M]), ALU.max))
                order.wait()
                if past(b, 1):
                    dve.wait_ge(mask_rows, Q * (b - 1) + 2 * g + 2)
                v.tensor_scalar(mask[g][:], kept2[:], -1.0, -MASKED / 2, ALU.add, ALU.mult).then_inc(mask_ready, 1)

            def maxes(u, i, g):
                for t in range(TB):
                    n = G * TB * u + TB * g + t
                    dve.wait_ge(s_in_psum, n + 1)
                    if g == 0 and t == 0 and past(u, 2):
                        dve.wait_ge(top_in_psum, u - 1)
                    v.tensor_reduce(top[i][:, TB * g + t:TB * g + t + 1], ps_s[t % 2][:], AX, ALU.max).then_inc(s_max, 1)

            def take_top(u, q):
                i = q % 2
                dve.wait_ge(top_in_psum, u + 1)
                if past(u, 2):
                    dve.wait_ge(top_here[i], top_rows_before(u))
                v.tensor_copy(top_part[i][0][:], ps_m[0:G * TB, 0, :]).then_inc(top_high, 1)
                dve.wait_ge(top_high, u + 1)
                v.tensor_tensor(top_part[i][1][:], ps_m[0:G * TB, 0, :], f32(top_part[i][0][:]),
                                ALU.subtract).then_inc(top_low, 1)

            batch = [None]

            def top_rows_before(u):
                if isinstance(u, int):
                    return 32 * (u // 2)
                b, q = batch[0]
                return (2 * b + q // 2) * 32

            def take_o(u, q):
                dve.wait_ge(ot_in_psum, u + 1)
                o = ps_m[:].rearrange("p t (g c) -> p t g c", g=G)
                if past(u, 1):
                    dve.wait_ge(on_ready, u)
                v.reciprocal(rec[:], o[:, :, :, HD]).then_inc(rec_ready, 1)
                dve.wait_ge(rec_ready, u + 1)
                if q == 0 and past(u, 4):
                    dve.wait_ge(on_in_psum, KD * batch_of_o[0])
                v.tensor_tensor(on[:, :, q * G * HD:(q + 1) * G * HD].rearrange("p t (g d) -> p t g d", g=G),
                                o[:, :, :, 0:HD], rec[:].unsqueeze(3).broadcast_to([P, TB, G, HD]),
                                ALU.mult).then_inc(on_ready, 1)

            batch_of_o = [None]

            def add_y(b):
                dve.wait_ge(part_here, 16 * b + 16)
                dve.wait_ge(y_here, 2 * TB * 16 * (b + 1))
                for j in range(2):
                    if j:
                        dve.wait_ge(added, 2 * TB * b + TB)
                    for t in range(TB):
                        v.scalar_tensor_tensor(out=part[:, t, :], in0=yg[j][:, t, :],
                                               scalar=keep["weight"][:, j, bass.ds(TB * b + t, 1)], in1=part[:, t, :],
                                               op0=ALU.mult, op1=ALU.add).then_inc(added, 1)

            def finish(b):
                add_y(b)
                for c in range(KD):
                    dve.wait_ge(on_high, KD * b + c + 1)
                    v.tensor_tensor(on_part[1][:, c, :], ps_s[c][:], f32(on_part[0][:, c, :]),
                                    ALU.subtract).then_inc(on_low, 1)
                dve.wait_ge(added, 2 * TB * (b + 1))
                for o in range(2):
                    dve.wait_ge(fin_in_psum, 2 * b + o + 1)
                    v.tensor_tensor(part[:, 2 * o:2 * o + 2, :].rearrange("p t d -> p (t d)"), ps_s[o][:],
                                    part[:, 2 * o:2 * o + 2, :].rearrange("p t d -> p (t d)"), ALU.add).then_inc(fin_ready, 1)

            def stage_of(b, q, with_s, with_top):
                u = Q * b + q
                for g in range(G):
                    if with_s:
                        maxes(u + 2, q % 2, g)
                    if g == 1 and with_top:
                        batch[0] = (b, q + 1)
                        take_top(u + 1, (q + 1) % Q)
                    if g == 2 and (past(b, 1) or q >= 2):
                        batch_of_o[0] = b
                        take_o(u - 2, (q - 2) % Q)

            def scores_ahead(b):
                for j in range(2 * KD):
                    take_qk(b, j)
                    if j % 2:
                        own_k(b, j // 2)
                for g in range(KD):
                    select(b, g)

            scores_ahead(0)
            for g in range(G):
                maxes(0, 0, g)
            take_top(0, 0)
            for g in range(G):
                maxes(1, 1, g)

            def body(b, first=False, last=False):
                stage_of(b, 0, True, True)
                stage_of(b, 1, True, True)
                if not last:
                    scores_ahead(b + 1)
                if not first:
                    finish(b - 1)
                stage_of(b, 2, not last, True)
                stage_of(b, 3, not last, not last)

            batches(dve, body)
            for q in (2, 3):
                take_o(Q * (B - 1) + q, q)
            finish(B - 1)

        @block.tensor
        def _(pe):
            pe.wait_ge(w_low, 1)
            pe.wait_ge(consts, 2)
            pe.wait_ge(const_rows, 16 * Q)

            def qk(b, j):
                g, s = j // 2, j % 2
                cols = slice(s * D + g * P, s * D + (g + 1) * P)
                exact_products(nc, ps_s[s][:],
                               [[w_part[x][:, k, cols] for x in range(2)] for k in range(KD)],
                               [[(xh, xl)[x][:, k, :] for x in range(2)] for k in range(KD)]).then_inc(qk_in_psum, 1)

            def block_scores(b, g):
                pe.wait_ge(k_own_ready, KD * b + g + 1)
                nc.tensor.matmul(ps_m[0:M, 0, 0:HG * M], qk_sum[0][g][:], k_own[:].rearrange("p h m -> p (h m)"),
                                 start=True, stop=True).then_inc(c_in_psum, 1)

            def scores_ahead(b, first=False):
                pe.wait_ge(xl_ready, b + 1)
                for j in range(2 * KD):
                    if j >= 2:
                        pe.wait_ge(qk_taken, 2 * KD * b + j - 1)
                    elif not first:
                        pe.wait_ge(s_max, G * TB * Q * b)
                    qk(b, j)
                    if j == 2 * KD - 2:
                        if not first:
                            pe.wait_ge(on_ready, Q * (b - 1))
                        block_scores(b, 0)
                pe.wait_ge(mask_ready, KD * b + 1)
                block_scores(b, 1)

            def s_pass(u, b, q, g, banks=None):
                if g == 0:
                    pe.wait_ge(stack_here[q], 128 * b + 128)
                    pe.wait_ge(mask_rows, u + 1)
                for t in range(TB):
                    n = G * TB * u + TB * g + t
                    if g == 0 and t < 2 and banks is not None:
                        pe.wait_ge(banks[0], banks[1][t])
                    elif past(n, 2) or not isinstance(n, int):
                        pe.wait_ge(s_max, n - 1)
                    nc.tensor.matmul(ps_s[t % 2][:], stack[0][q][0:TOP0, g, t * P:(t + 1) * P],
                                     stack[1][q][0:TOP0, g, :], start=True, stop=True).then_inc(s_in_psum, 1)

            def top_by_query(u, q, waits):
                pe.wait_ge(s_max, G * TB * (u + 1))
                for w in waits:
                    pe.wait_ge(*w)
                nc.tensor.transpose(ps_m[0:G * TB, 0, :], top[q % 2][:], keep["ident"][:]).then_inc(top_in_psum, 1)

            def st_pass(u, b, q, g):
                if g == 0:
                    pe.wait_ge(top_here[q % 2], 64 * b + 32 * (q // 2) + 32)
                for half in range(2):
                    n = 2 * G * u + 2 * g + half
                    if past(n, 2):
                        pe.wait_ge(exp_ready, n - 1)
                    for t in (2 * half, 2 * half + 1):
                        last = nc.tensor.matmul(ps_st[half][:, t % 2, :], stack[1][q][:, g, t * P:(t + 1) * P],
                                                stack[0][q][:, g, :], start=True, stop=True)
                    last.then_inc(st_in_psum, 1)

            def pv(u, q, t):
                if t == 0:
                    pe.wait_ge(exp_ready, 2 * G * (u + 1))
                    if past(u, 1):
                        pe.wait_ge(pv_ready, u)
                for g in range(G):
                    last = nc.tensor.matmul(ps_pv[2 * HD * g:2 * HD * (g + 1), :], vx[:, t, G * q + g, :],
                                            pt[q % 2][:, g, t, :], start=(t == 0), stop=(t == TB - 1))
                if t == TB - 1:
                    last.then_inc(pv_in_psum, 1)

            def o_by_token(u, waits):
                pe.wait_ge(pv_ready, u + 1)
                for w in waits:
                    pe.wait_ge(*w)
                for t in range(TB):
                    last = nc.tensor.transpose(ps_m[:, t, :], o_unit[:, t * P:(t + 1) * P], keep["ident"][:])
                last.then_inc(ot_in_psum, 1)

            def values(b):
                pe.wait_ge(s_max, G * TB * (Q * b + 3))
                for o in range(2):
                    for t in (2 * o, 2 * o + 1):
                        last = exact_products(
                            nc, ps_s[o][:, (t % 2) * D:(t % 2 + 1) * D],
                            [[(xh, xl)[x][:, k, t * P:(t + 1) * P] for x in range(2)] for k in range(KD)],
                            [[w_part[x][:, k, 2 * D:3 * D] for x in range(2)] for k in range(KD)])
                    last.then_inc(v_in_psum, 1)

            def project(b, bank_free):
                pe.wait_ge(on_ready, Q * (b + 1))
                for c in range(KD):
                    for w in bank_free[c]:
                        pe.wait_ge(*w)
                    for t in range(TB):
                        last = nc.tensor.transpose(ps_s[c][:, t * P:(t + 1) * P], on[:, t, c * P:(c + 1) * P],
                                                   keep["ident"][:])
                    last.then_inc(on_in_psum, 1)
                pe.wait_ge(on_low, KD * (b + 1))
                for o in range(2):
                    for t in (2 * o, 2 * o + 1):
                        last = exact_products(
                            nc, ps_s[o][:, (t % 2) * D:(t % 2 + 1) * D],
                            [[on_part[x][:, c, t * P:(t + 1) * P] for x in range(2)] for c in range(KD)],
                            [[wp_part[x][:, c, :] for x in range(2)] for c in range(KD)])
                    last.then_inc(fin_in_psum, 1)

            def stage_of(b, q, with_s, with_top, banks=None, top_waits=()):
                u = Q * b + q
                for g in range(G):
                    st_pass(u, b, q, g)
                    if with_s:
                        s_pass(u + 2, b if q < 2 else b + 1, (q + 2) % Q, g, banks)
                    if past(u, 1):
                        pv(u - 1, (q - 1) % Q, g)
                    if g == 1 and with_top:
                        top_by_query(u + 1, (q + 1) % Q, top_waits)
                    if g == 2 and (past(b, 1) or q >= 2):
                        waits = [(top_low, u + 2)] if with_top else [(on_ready, u - 2)]
                        o_by_token(u - 2, waits)

            scores_ahead(0, first=True)
            for g in range(G):
                s_pass(0, 0, 0, g, banks=(qk_taken, (2 * KD - 1, 2 * KD)) if g == 0 else None)
            top_by_query(0, 0, [(mask_ready, KD)])
            for g in range(G):
                s_pass(1, 0, 1, g)

            def body(b, first=False, last=False):
                used = [(top_low, 1)] if first else [(on_ready, Q * b - 3)]
                stage_of(b, 0, True, True, None, used)
                values(b)
                used = [(top_low, Q * b + 2)] if first else [(on_ready, Q * b - 2)]
                stage_of(b, 1, True, True, (v_ready, (2 * b + 1, 2 * b + 2)), used)
                if not last:
                    scores_ahead(b + 1, first=False)
                if not first:
                    if last:
                        free = [[(s_max, G * TB * Q * (b + 1))]] * 2
                    else:
                        free = [[(qk_taken, 2 * KD * (b + 1) + 2 * KD - 1 + c)] for c in range(KD)]
                    project(b - 1, free)
                if first:
                    banks = (qk_taken, (2 * KD * (b + 1) + 2 * KD - 1, 2 * KD * (b + 1) + 2 * KD))
                    used = [(mask_ready, KD * (b + 2))]
                else:
                    banks = (fin_ready, (2 * b - 1, 2 * b))
                    used = [(on_ready, Q * b)] if last else [(mask_ready, KD * (b + 2))]
                stage_of(b, 2, not last, True, banks, used)
                stage_of(b, 3, not last, not last, None, [(on_ready, Q * b + 1)])

            batches(pe, body)
            U = Q * B
            for t in range(TB):
                pv(U - 1, Q - 1, t)
            for u in (U - 2, U - 1):
                o_by_token(u, [(on_ready, u)])
            project(B - 1, [[(fin_ready, 2 * (B - 1) - 1 + c)] for c in range(KD)])


def build(nc, x, qkv_wT, proj_wT, proj_b, Wr, Wg, Wu, Wd, Sg, Su, Sd, out, phases=9):
    sh = Shapes(x, qkv_wT, Wr, Wg, Sg)
    dram = dict(x=x, qkv_wT=qkv_wT, proj_wT=proj_wT, proj_b=proj_b, Wr=Wr, Wg=Wg, Wu=Wu, Wd=Wd, Sg=Sg, Su=Su,
                Sd=Sd, out=out)

    def scratch(name, shape, dt=F32):
        dram[name] = nc.dram_tensor(f"scratch_{name}", list(shape), dt, kind="Internal").ap()

    slots = sh.SLOT_TILES * P
    scratch("xn", [sh.T, sh.D])
    scratch("xT", [sh.B, P, sh.KD, sh.N])
    scratch("part", [sh.T, sh.D])
    scratch("table", [slots, 1], I32)
    scratch("y", [slots, sh.D])
    scratch("qkT", [sh.B, 2, sh.KD, 2, P, sh.N])
    with ExitStack() as ctx:
        def sb(name, shape, dt=F32):
            return ctx.enter_context(nc.sbuf_tensor(name, shape, dt))

        keep = dict(
            ident=sb("ident", [P, P]),
            slot=sb("slot", [P, 2, sh.NT], I32),
            place=sb("place", [P, 2, sh.NT], I32),
            token=sb("token", [P, sh.NT], I32),
            weight=sb("weight", [P, 2, sh.NT]),
            experts=sb("experts", [1, sh.SLOT_TILES // 2 + sh.DOWN_LAG], I32),
        )
        with ExitStack() as inner:
            keep["xT"] = inner.enter_context(nc.sbuf_tensor("xT_all", [P, sh.KD, sh.T], F32))
            phase_route(nc, sh, dram, keep)
            if phases >= 2:
                phase_shared(nc, sh, dram, keep)
        if phases >= 3:
            phase_experts(nc, sh, dram, keep)
        if phases >= 4:
            phase_attention(nc, sh, dram, keep)


def kernel(L0_attn_x, L0_attn_qkv_w, L0_attn_proj_w, L0_attn_proj_b, L0_ffn_Wr, L0_ffn_Wg, L0_ffn_Wu, L0_ffn_Wd,
           L0_ffn_Sg, L0_ffn_Su, L0_ffn_Sd):
    import numpy as np
    import concourse.bacc as bacc
    from concourse.bass_utils import run_bass_kernel_spmd

    arrays = dict(x=L0_attn_x, qkv_wT=np.asarray(L0_attn_qkv_w).T, proj_wT=np.asarray(L0_attn_proj_w).T,
                  proj_b=np.asarray(L0_attn_proj_b).reshape(1, -1), Wr=L0_ffn_Wr, Wg=L0_ffn_Wg, Wu=L0_ffn_Wu,
                  Wd=L0_ffn_Wd, Sg=L0_ffn_Sg, Su=L0_ffn_Su, Sd=L0_ffn_Sd)
    arrays = {f"in_{n}": np.ascontiguousarray(a) for n, a in arrays.items()}
    nc = bacc.Bacc("TRN2", target_bir_lowering=False, num_devices=1)
    args = [nc.dram_tensor(n, a.shape, mybir.dt.from_np(a.dtype), kind="ExternalInput").ap()
            for n, a in arrays.items()]
    args.append(nc.dram_tensor("out", arrays["in_x"].shape, F32, kind="ExternalOutput").ap())
    build(nc, *args)
    return run_bass_kernel_spmd(nc, [arrays], core_ids=[0]).results[0]["out"]
```

```python
from contextlib import ExitStack

import concourse.bass as bass
from concourse import mybir

ALU = mybir.AluOpType
ACT = mybir.ActivationFunctionType
AX = mybir.AxisListType.X
F32 = mybir.dt.float32
F32R = mybir.dt.float32r
I32 = mybir.dt.int32

P = 128
MASKED = -float(2 ** 100)
LN_EPS = 1e-5


class Order:

    def __init__(self, engine, sem, base=0):
        self.engine, self.sem, self.base, self.n = engine, sem, base, 0

    def done(self, instruction):
        self.n += 1
        instruction.then_inc(self.sem, 1)

    def wait(self):
        self.engine.wait_ge(self.sem, self.base + self.n)


def f32(ap):
    return ap.bitcast(F32)


class Shapes:

    def __init__(self, x, qkv_wT, Wr, Wg, Sg):
        self.B, self.N, self.D = x.shape
        self.T = self.B * self.N
        self.KD = self.D // P
        self.TB = self.N // P
        self.NT = self.T // P
        self.E, _, self.F = Wg.shape
        self.FS = Sg.shape[1]
        self.H, self.HD = 16, self.D // 16
        self.BS = 64
        self.M = self.N // self.BS
        self.TOPK = 2
        most = (self.TOPK * self.T + self.E * (P - 1)) // P
        self.SLOT_TILES = most + most % 2
        self.GATE_LAG, self.DOWN_LAG = 1, 3


def phase_route(nc, sh, dram, keep):
    B, N, D, KD, TB, NT, E = sh.B, sh.N, sh.D, sh.KD, sh.TB, sh.NT, sh.E
    ST = sh.SLOT_TILES
    with ExitStack() as ctx:
        def sb(name, shape, dt=F32):
            return ctx.enter_context(nc.sbuf_tensor(name, shape, dt))

        def ps(name, shape=(P, 512)):
            return ctx.enter_context(nc.psum_tensor(name, list(shape), F32))

        def sem(name):
            return ctx.enter_context(nc.semaphore(name))

        x_in = [sb(f"x_in{i}", [P, TB, D]) for i in range(2)]
        xn = [sb(f"xn{i}", [P, TB, D]) for i in range(2)]
        bn6 = [sb(f"bn6_{i}", [P, TB, 6]) for i in range(2)]
        mean = [sb(f"mean{i}", [P, TB]) for i in range(2)]
        msum = [sb(f"msum{i}", [P, TB]) for i in range(2)]
        dif = [sb(f"dif{i}", [P, TB]) for i in range(2)]
        dif2 = [sb(f"dif2_{i}", [P, TB]) for i in range(2)]
        m2 = [sb(f"m2_{i}", [P, TB]) for i in range(2)]
        var = [sb(f"var{i}", [P, TB]) for i in range(2)]
        vare = [sb(f"vare{i}", [P, TB]) for i in range(2)]
        rstd = [sb(f"rstd{i}", [P, TB]) for i in range(2)]
        minus_half = sb("minus_half", [P, TB])
        wr = sb("wr", [P, KD, E])
        logitT = [sb(f"logitT{i}", [P, N]) for i in range(2)]
        logit = sb("logit", [P, NT, E])

        CH = NT * E // 512
        by_expert, small, per_tile = [P, NT, E], [P, E], [P, NT]
        route = {name: sb(f"route_{name}", shape) for name, shape in dict(
            top0=per_tile, top1=per_tile, first0=per_tile, first1=per_tile, below2=per_tile, exp2=per_tile,
            sum=per_tile, hot0=by_expert, hot1=by_expert, equal=by_expert, cand=by_expert, rest=by_expert,
            below=by_expert, exps=by_expert, pairs=[P, NT * E], all=[P, NT * E], upto=[P, NT * E],
            ahead=[P, NT * E], ahead2=[P, NT * E], slot_et=[P, NT * E], one=[P, NT * E], count=small,
            tiles=small, end=small, begin=small, base=small, iota_e=small, slot=[P, 2, NT], iota_j=[1, ST],
            expert=[1, ST], pair=[1, ST // 2 + 2 * sh.DOWN_LAG], ended=[1, ST, E]).items()}
        route |= {name: sb(f"route_{name}", shape, I32) for name, shape in dict(
            count_i=small, tiles_i=small, lane=[P, 2, NT], tile=[P, 2, NT], iota_ei=small,
            iota_ji=[1, ST]).items()}
        before = sb("before", [P, P])
        ones = sb("ones", [P, P])
        table_zero = sb("table_zero", [P, ST], I32)

        ps_xT = [[ps(f"ps_xT{i}_{k}") for k in range(KD)] for i in range(2)]
        ps_lT = [ps(f"ps_lT{i}") for i in range(2)]
        ps_l = [ps(f"ps_l{i}") for i in range(2)]

        ps_all, ps_before = ps_xT[0][0:2], ps_xT[1][0:2]
        iota_made = sem("iota_made")
        pairs_ready = sem("pairs_ready")
        below_ready = sem("below_ready")
        exp_ready = sem("exp_ready")
        counts_in_psum = sem("counts_in_psum")
        x_here = [sem(f"x_here{i}") for i in range(2)]
        xn_stored = [sem(f"xn_stored{i}") for i in range(2)]
        table_zeroed = sem("table_zeroed")
        wr_here = sem("wr_here")
        const_made = sem("const_made")
        ident_made = sem("ident_made")
        dve_order = sem("dve_order")
        var_ready = sem("var_ready")
        rstd_ready = sem("rstd_ready")
        xn_ready = sem("xn_ready")
        xT_in_psum = sem("xT_in_psum")
        xT_ready = sem("xT_ready")
        lT_in_psum = sem("lT_in_psum")
        lT_ready = sem("lT_ready")
        l_in_psum = sem("l_in_psum")
        l_ready = sem("l_ready")

        xn_tok = dram["xn"].rearrange("(b t p) d -> b p t d", p=P, t=TB)
        x_tok = dram["x"].rearrange("b (t p) d -> b p t d", p=P)
        one = lambda ap: ap.rearrange("o p t d -> (o p) t d")
        block = ctx.enter_context(nc.Block())
        HB = B // 2

        @block.sync
        def _(sp):
            sp.dma_start(wr[:], dram["Wr"].rearrange("(k p) e -> p k e", p=P)).then_inc(wr_here, 16)
            for i in range(2):
                sp.dma_start(x_in[i][:], one(x_tok[i:i + 1])).then_inc(x_here[i], 16)

            sp.wait_ge(iota_made, 10)
            sp.dma_start(dram["table"].rearrange("(p j) o -> p (j o)", p=P), table_zero[:]).then_inc(table_zeroed, 16)

            def step(b, i, load):
                ready, at, nxt = sp.snap(b + 1), sp.snap(b), sp.snap(b + 2)
                sp.wait_ge(xn_ready, ready)
                sp.dma_start(one(xn_tok[bass.ds(at, 1)]), xn[i][:]).then_inc(xn_stored[i], 16)
                if load:
                    sp.dma_start(x_in[i][:], one(x_tok[bass.ds(nxt, 1)])).then_inc(x_here[i], 16)

            with sp.Fori(0, HB - 1) as h:
                for i in range(2):
                    step(2 * h + i, i, True)
            for i in range(2):
                step(B - 2 + i, i, False)
            for i in range(2):
                sp.wait_ge(xn_stored[i], 16 * HB)
            sp.wait_ge(table_zeroed, 16)

        def route_pairs(order):
            v, r = nc.vector, route

            def do(instruction):
                order.done(instruction)
                order.wait()

            def over_e(ap):
                return ap.unsqueeze(2).broadcast_to([P, NT, E])

            def over_t(ap):
                return ap.unsqueeze(1).broadcast_to([P, NT, E])

            iota_e = over_t(r["iota_e"][:])
            left = logit
            for j in range(2):
                top, first, hot = r[f"top{j}"], r[f"first{j}"], r[f"hot{j}"]
                do(v.tensor_reduce(top[:], left[:], AX, ALU.max))
                do(v.tensor_tensor(r["equal"][:], left[:], over_e(top[:]), ALU.is_equal))
                do(v.scalar_tensor_tensor(out=r["cand"][:], in0=r["equal"][:], scalar=-float(E), in1=iota_e,
                                          op0=ALU.mult, op1=ALU.add))
                do(v.tensor_reduce(first[:], r["cand"][:], AX, ALU.min))
                do(v.tensor_tensor(hot[:], r["cand"][:], over_e(first[:]), ALU.is_equal))
                if j == 0:
                    do(v.scalar_tensor_tensor(out=r["rest"][:], in0=hot[:], scalar=-3e38, in1=logit[:],
                                              op0=ALU.mult, op1=ALU.add))
                    left = r["rest"]
            v.tensor_tensor(r["pairs"][:].rearrange("p (e t) -> p t e", e=E), r["hot0"][:], r["hot1"][:],
                            ALU.add).then_inc(pairs_ready, 1)
            v.tensor_tensor(r["below2"][:], r["top1"][:], r["top0"][:], ALU.subtract)
            v.tensor_tensor(r["below"][:], logit[:], over_e(r["top0"][:]), ALU.subtract).then_inc(below_ready, 1)

            order.engine.wait_ge(counts_in_psum, 1)
            for c in range(CH):
                order.done(v.tensor_copy(r["all"][:, c * 512:(c + 1) * 512], ps_all[c][:]))
            order.wait()
            do(v.tensor_tensor_scan(r["upto"][:], r["one"][:], r["all"][:], 0.0, ALU.mult, ALU.add))
            do(v.tensor_tensor(r["ahead"][:], r["upto"][:], r["all"][:], ALU.subtract))
            upto, ahead = (r[n][:].rearrange("p (e t) -> p e t", e=E) for n in ("upto", "ahead"))
            do(v.tensor_tensor(r["count"][:], upto[:, :, NT - 1], ahead[:, :, 0], ALU.subtract))
            do(v.tensor_scalar(r["count_i"][:], r["count"][:], float(P - 1), None, ALU.add))
            do(v.tensor_scalar(r["tiles_i"][:], r["count_i"][:], 7, None, ALU.logical_shift_right))
            do(v.tensor_copy(r["tiles"][:], r["tiles_i"][:]))
            do(v.tensor_tensor_scan(r["end"][:], r["one"][:, 0:E], r["tiles"][:], 0.0, ALU.mult, ALU.add))
            do(v.tensor_tensor(r["begin"][:], r["end"][:], r["tiles"][:], ALU.subtract))
            do(v.scalar_tensor_tensor(out=r["base"][:], in0=r["begin"][:], scalar=float(P), in1=ahead[:, :, 0],
                                      op0=ALU.mult, op1=ALU.subtract))
            for c in range(CH):
                order.done(v.tensor_tensor(r["ahead2"][:, c * 512:(c + 1) * 512], ps_before[c][:],
                                           r["ahead"][:, c * 512:(c + 1) * 512], ALU.add))
            order.wait()
            do(v.tensor_tensor(r["slot_et"][:].rearrange("p (e t) -> p e t", e=E),
                               r["ahead2"][:].rearrange("p (e t) -> p e t", e=E),
                               r["base"][:].unsqueeze(2).broadcast_to([P, E, NT]), ALU.add))
            slot_te = r["slot_et"][:].rearrange("p (e t) -> p t e", e=E)
            for j in range(2):
                do(v.tensor_tensor(r["cand"][:], slot_te, r[f"hot{j}"][:], ALU.mult))
                do(v.tensor_reduce(r["slot"][:, j, :], r["cand"][:], AX, ALU.add))
            do(v.tensor_copy(keep["slot"][:], r["slot"][:]))
            order.done(v.tensor_scalar(r["lane"][:], keep["slot"][:], P - 1, None, ALU.bitwise_and))
            order.done(v.tensor_scalar(r["tile"][:], keep["slot"][:], 7, None, ALU.logical_shift_right))
            order.wait()
            do(v.scalar_tensor_tensor(out=keep["place"][:], in0=r["lane"][:], scalar=float(ST), in1=r["tile"][:],
                                      op0=ALU.mult, op1=ALU.add))
            do(v.tensor_tensor(r["ended"][:], r["end"][0:1, :].unsqueeze(1).broadcast_to([1, ST, E]),
                               r["iota_j"][:].unsqueeze(2).broadcast_to([1, ST, E]), ALU.is_le))
            do(v.tensor_reduce(r["expert"][:], r["ended"][:], AX, ALU.add))
            do(v.tensor_scalar(r["expert"][:], r["expert"][:], float(E - 1), None, ALU.min))
            by_pair = r["expert"][:].rearrange("o (q u) -> o q u", u=2)
            Q, G, W = ST // 2, sh.GATE_LAG, sh.DOWN_LAG
            do(v.scalar_tensor_tensor(out=r["pair"][:, W:W + Q], in0=by_pair[:, :, 1], scalar=float(E),
                                      in1=by_pair[:, :, 0], op0=ALU.mult, op1=ALU.add))
            do(v.scalar_tensor_tensor(out=keep["experts"][:], in0=r["pair"][:, 0:Q + W], scalar=float(E * E),
                                      in1=r["pair"][:, W - G:W - G + Q + W], op0=ALU.mult, op1=ALU.add))
            order.engine.wait_ge(exp_ready, 1)
            do(v.tensor_reduce(r["sum"][:], r["exps"][:], AX, ALU.add))
            do(v.reciprocal(keep["weight"][:, 0, :], r["sum"][:]))
            do(v.tensor_tensor(keep["weight"][:, 1, :], keep["weight"][:, 0, :], r["exp2"][:], ALU.mult))

        @block.gpsimd
        def _(pool):
            nc.gpsimd.iota(keep["token"][:], pattern=[[P, NT]], base=0, channel_multiplier=1).then_inc(iota_made, 1)
            nc.gpsimd.iota(route["iota_ei"][:], pattern=[[1, E]], base=0, channel_multiplier=0).then_inc(iota_made, 1)
            nc.gpsimd.iota(route["iota_ji"][:], pattern=[[1, ST]], base=0, channel_multiplier=0).then_inc(iota_made, 1)
            nc.gpsimd.memset(route["one"][:], 1.0).then_inc(iota_made, 1)
            nc.gpsimd.memset(route["pair"][:], 0.0).then_inc(iota_made, 1)
            nc.gpsimd.memset(table_zero[:], 0).then_inc(iota_made, 1)
            for i in range(2):
                nc.gpsimd.memset(logitT[i][:], 0.0).then_inc(iota_made, 1)
            pool.wait_ge(iota_made, 8)
            nc.gpsimd.tensor_copy(route["iota_e"][:], route["iota_ei"][:]).then_inc(iota_made, 1)
            nc.gpsimd.tensor_copy(route["iota_j"][:], route["iota_ji"][:]).then_inc(iota_made, 1)
            nc.gpsimd.memset(minus_half[:], -0.5).then_inc(const_made, 1)
            nc.gpsimd.memset(keep["ident"][:], 0.0).then_inc(ident_made, 1)
            nc.gpsimd.memset(before[:], 1.0).then_inc(ident_made, 1)
            nc.gpsimd.memset(ones[:], 1.0).then_inc(ident_made, 1)
            pool.wait_ge(ident_made, 3)
            nc.gpsimd.affine_select(out=keep["ident"][:], in_=keep["ident"][:], compare_op=ALU.not_equal, fill=1.0,
                                    base=0, pattern=[[-1, P]], channel_multiplier=1).then_inc(ident_made, 1)
            nc.gpsimd.affine_select(out=before[:], in_=before[:], compare_op=ALU.is_gt, fill=0.0,
                                    base=0, pattern=[[1, P]], channel_multiplier=-1).then_inc(ident_made, 1)
            pool.wait_ge(const_made, 1)

            def step(b, i):
                pool.wait_ge(var_ready, b + 1)
                nc.gpsimd.tensor_tensor(rstd[i][:], vare[i][:], minus_half[:], ALU.pow).then_inc(rstd_ready, 1)

            with pool.Fori(0, HB) as h:
                for i in range(2):
                    step(2 * h + i, i)

        @block.vector
        def _(dve):
            ORDERED = 4

            def stats(b, h, i):
                order = Order(dve, dve_order, b * ORDERED)
                dve.wait_ge(x_here[i], 16 * h + 16)
                for t in range(TB):
                    last = nc.vector.bn_stats(bn6[i][:, t, :], x_in[i][:, t, :])
                order.done(last)
                order.wait()
                s = bn6[i]
                nc.vector.tensor_tensor(dif[i][:], s[:, :, 1], s[:, :, 4], ALU.subtract)
                nc.vector.tensor_tensor(msum[i][:], s[:, :, 1], s[:, :, 4], ALU.add)
                order.done(nc.vector.tensor_tensor(m2[i][:], s[:, :, 2], s[:, :, 5], ALU.add))
                order.wait()
                nc.vector.tensor_scalar(mean[i][:], msum[i][:], 0.5, None, ALU.mult)
                order.done(nc.vector.tensor_tensor(dif2[i][:], dif[i][:], dif[i][:], ALU.mult))
                order.wait()
                order.done(nc.vector.scalar_tensor_tensor(out=var[i][:], in0=dif2[i][:], scalar=D / 4.0,
                                                          in1=m2[i][:], op0=ALU.mult, op1=ALU.add))
                order.wait()
                nc.vector.tensor_scalar(vare[i][:], var[i][:], 1.0 / D, LN_EPS, ALU.mult, ALU.add).then_inc(var_ready, 1)
                assert order.n == ORDERED

            def norm(b, h, i, first):
                dve.wait_ge(rstd_ready, b + 1)
                if not first:
                    dve.wait_ge(xT_in_psum, b - 1)
                    dve.wait_ge(xn_stored[i], 16 * h)
                for t in range(TB):
                    last = nc.vector.tensor_scalar(xn[i][:, t, :], x_in[i][:, t, :], mean[i][:, t:t + 1],
                                                   rstd[i][:, t:t + 1], ALU.subtract, ALU.mult)
                last.then_inc(xn_ready, 1)

            def take_logits(b, i):
                dve.wait_ge(l_in_psum, b + 1)
                nc.vector.tensor_copy(logit[:, bass.ds(b * TB, TB), :],
                                      ps_l[i][:].rearrange("p (t e) -> p t e", t=TB)[:, :, 0:E]).then_inc(l_ready, 1)

            LAG = 2
            dve.wait_ge(iota_made, 10)
            for b in range(LAG):
                stats(b, b // 2, b % 2)
                norm(b, b // 2, b % 2, True)
            with dve.Fori(1, HB) as h:
                for i in range(2):
                    stats(2 * h + i, h, i)
                    norm(2 * h + i, h, i, False)
                    take_logits(2 * h + i - LAG, i)
            for b in range(B - LAG, B):
                take_logits(b, b % 2)
            dve.wait_ge(l_ready, B)
            route_pairs(Order(dve, dve_order, B * ORDERED))

        @block.tensor
        def _(pe):
            pe.wait_ge(ident_made, 5)
            pe.wait_ge(wr_here, 16)

            def transpose_x(b, i, first):
                pe.wait_ge(xn_ready, b + 1)
                if not first:
                    pe.wait_ge(xT_ready, 2 * b - 2)
                for k in range(KD):
                    for t in range(TB):
                        last = nc.tensor.transpose(ps_xT[i][k][:, t * P:(t + 1) * P],
                                                   xn[i][:, t, k * P:(k + 1) * P], keep["ident"][:])
                last.then_inc(xT_in_psum, 1)

            def router(b, i, first):
                pe.wait_ge(xT_ready, 2 * b + 2)
                if not first:
                    pe.wait_ge(lT_ready, b - 1)
                for k in range(KD):
                    last = nc.tensor.matmul(ps_lT[i][0:E, :], wr[:, k, :], keep["xT"][:, k, bass.ds(b * N, N)],
                                            start=(k == 0), stop=(k == KD - 1))
                last.then_inc(lT_in_psum, 1)

            def logits_by_token(b, i, first):
                pe.wait_ge(lT_ready, b + 1)
                if not first:
                    pe.wait_ge(l_ready, b - 1)
                for t in range(TB):
                    last = nc.tensor.transpose(ps_l[i][:, t * P:(t + 1) * P], logitT[i][:, t * P:(t + 1) * P],
                                               keep["ident"][:])
                last.then_inc(l_in_psum, 1)

            def step(b, i):
                if not (isinstance(b, int) and b < 2):
                    logits_by_token(b - 2, i, isinstance(b, int) and b < 4)
                if not (isinstance(b, int) and b < 1):
                    router(b - 1, 1 - i, isinstance(b, int) and b < 3)
                if not (isinstance(b, int) and b >= B):
                    transpose_x(b, i, isinstance(b, int) and b < 2)

            for b in range(4):
                step(b, b % 2)
            with pe.Fori(2, HB) as h:
                for i in range(2):
                    step(2 * h + i, i)
            logits_by_token(B - 2, 0, False)
            router(B - 1, 1, False)
            logits_by_token(B - 1, 1, False)
            pe.wait_ge(pairs_ready, 1)
            for c in range(CH):
                cols = slice(c * 512, (c + 1) * 512)
                nc.tensor.matmul(ps_before[c][:], before[:], route["pairs"][:, cols], start=True, stop=True)
                last = nc.tensor.matmul(ps_all[c][:], ones[:], route["pairs"][:, cols], start=True, stop=True)
            last.then_inc(counts_in_psum, 1)

        @block.scalar
        def _(act):
            def copy_xT(b, i):
                act.wait_ge(xT_in_psum, b + 1)
                for k in range(KD):
                    nc.scalar.copy(keep["xT"][:, k, bass.ds(b * N, N)], ps_xT[i][k][:]).then_inc(xT_ready, 1)

            def copy_lT(b, i, first):
                act.wait_ge(lT_in_psum, b + 1)
                if not first:
                    act.wait_ge(l_in_psum, b - 1)
                nc.scalar.copy(logitT[i][0:E, :], ps_lT[i][0:E, :]).then_inc(lT_ready, 1)

            copy_xT(0, 0)
            copy_xT(1, 1)
            act.wait_ge(iota_made, 10)
            copy_lT(0, 0, True)
            copy_xT(2, 0)
            copy_lT(1, 1, True)
            copy_xT(3, 1)
            copy_lT(2, 0, False)
            with act.Fori(2, HB) as h:
                for i in range(2):
                    copy_xT(2 * h + i, i)
                    copy_lT(2 * h + i - 1, 1 - i, False)
            copy_lT(B - 1, 1, False)
            act.wait_ge(below_ready, 1)
            nc.scalar.activation(route["exps"][:], route["below"][:], ACT.Exp)
            nc.scalar.activation(route["exp2"][:], route["below2"][:], ACT.Exp).then_inc(exp_ready, 1)


def past(b, n):
    return not isinstance(b, int) or b >= n


def steps(engine, step, total, unroll=2, peeled=None, trailing=0):
    peeled = unroll if peeled is None else peeled
    for b in range(peeled):
        step(b, b % unroll)
    with engine.Fori(peeled // unroll, total // unroll) as h:
        for i in range(unroll):
            step(unroll * h + i, i)
    for b in range(total, total + trailing):
        step(b, b % unroll)


def exact_products(nc, out, lhs, rhs, first=True, last=True):
    todo = [(a[x], b[y]) for a, b in zip(lhs, rhs) for x, y in ((0, 0), (0, 1), (1, 0))]
    for n, (a, b) in enumerate(todo):
        ins = nc.tensor.matmul(out, a, b, start=(first and n == 0), stop=(last and n == len(todo) - 1))
    return ins


def phase_shared(nc, sh, dram, keep):
    B, N, D, KD, TB, NT, FS = sh.B, sh.N, sh.D, sh.KD, sh.TB, sh.NT, sh.FS
    KF = FS // P
    with ExitStack() as ctx:
        def sb(name, shape, dt=F32):
            return ctx.enter_context(nc.sbuf_tensor(name, shape, dt))

        def sem(name):
            return ctx.enter_context(nc.semaphore(name))

        def two(name, shape, dt=F32):
            return [sb(f"{name}{i}", shape, dt) for i in range(2)]

        w_in = sb("sh_w_in", [P, KD, 2, FS])
        wd_in = sb("sh_wd_in", [P, KF, D])
        w_part = [sb(f"sh_w_part{i}", [P, KD, 2, FS], F32R) for i in range(2)]
        wd_part = [sb(f"sh_wd_part{i}", [P, KF, D], F32R) for i in range(2)]
        bias = sb("sh_bias", [P, D])
        xh, xl = two("sh_xh", [P, KD, N], F32R), two("sh_xl", [P, KD, N], F32R)
        x_in = two("sh_x_in", [P, TB, D])
        xb = two("sh_xb", [P, TB, D])
        part = two("sh_part", [P, TB, D])
        th = [sb(f"sh_tanh{f}", [P, N]) for f in range(KF)]
        gs = [sb(f"sh_gs{f}", [P, N]) for f in range(KF)]
        hid = [sb(f"sh_hid{f}", [P, N]) for f in range(KF)]
        hh = [two(f"sh_hh{f}_", [P, N], F32R) for f in range(KF)]
        hl = [two(f"sh_hl{f}_", [P, N], F32R) for f in range(KF)]
        ps_gu = [[ctx.enter_context(nc.psum_tensor(f"sh_ps_gu{f}{g}", [P, N], F32)) for g in range(2)]
                 for f in range(KF)]
        ps_out = [ctx.enter_context(nc.psum_tensor(f"sh_ps_out{i}", [P, 2, D], F32)) for i in range(TB // 2)]

        w_here = sem("sh_w_here")
        w_high = sem("sh_w_high")
        w_low = sem("sh_w_low")
        x_here = [sem(f"sh_x_here{i}") for i in range(2)]
        xT_stored = sem("sh_xT_stored")
        part_stored = [sem(f"sh_part_stored{i}") for i in range(2)]
        xh_ready, xl_ready = sem("sh_xh_ready"), sem("sh_xl_ready")
        gu_in_psum = sem("sh_gu_in_psum")
        tanh_ready = sem("sh_tanh_ready")
        gs_ready = sem("sh_gs_ready")
        hid_ready = sem("sh_hid_ready")
        hh_ready, hl_ready = sem("sh_hh_ready"), sem("sh_hl_ready")
        out_in_psum = sem("sh_out_in_psum")
        xb_ready = sem("sh_xb_ready")
        part_ready = sem("sh_part_ready")
        staged = sem("sh_staged")
        in_table = [sem(f"sh_in_table{i}") for i in range(2)]

        x_tok = dram["x"].rearrange("b (t p) d -> b p t d", p=P)
        part_tok = dram["part"].rearrange("(b t p) d -> b p t d", p=P, t=TB)
        one = lambda ap: ap.rearrange("o p t d -> (o p) t d")
        block = ctx.enter_context(nc.Block())

        @block.sync
        def _(sp):
            for g, w in enumerate((dram["Sg"], dram["Su"])):
                sp.dma_start(w_in[:, :, g, :], w.rearrange("(k p) f -> p k f", p=P)).then_inc(w_here, 16)
            sp.dma_start(wd_in[:], dram["Sd"].rearrange("(k p) d -> p k d", p=P)).then_inc(w_here, 16)
            sp.dma_start(bias[:], dram["proj_b"].broadcast_to([P, D])).then_inc(w_here, 16)
            for i in range(2):
                sp.dma_start(x_in[i][:], one(x_tok[i:i + 1])).then_inc(x_here[i], 16)
            with sp.Fori(0, B) as b:
                at, col = sp.snap(b), sp.snap(b * N)
                sp.dma_start(one(dram["xT"][bass.ds(at, 1)]), keep["xT"][:, :, bass.ds(col, N)]).then_inc(xT_stored, 16)

            def step(b, i):
                ready, at = ((TB // 2) * (b + 1), b) if isinstance(b, int) else (sp.snap((b + 1) * (TB // 2)), sp.snap(b))
                sp.wait_ge(part_ready, ready)
                sp.dma_start(one(part_tok[bass.ds(at, 1)]), part[i][:]).then_inc(part_stored[i], 16)

            def load(b, i):
                used, at = sp.snap(b - 1), sp.snap(b)
                sp.wait_ge(xb_ready, used)
                sp.dma_start(x_in[i][:], one(x_tok[bass.ds(at, 1)])).then_inc(x_here[i], 16)

            with sp.Fori(1, B // 2) as h:
                for i in range(2):
                    load(2 * h + i, i)
                    step(2 * h + i - 2, i)
            for b in range(B - 2, B):
                step(b, b % 2)
            for i in range(2):
                sp.wait_ge(part_stored[i], 16 * (B // 2))
            sp.wait_ge(xT_stored, 16 * B)

        @block.gpsimd
        def _(pool):
            G = 4
            stage_place = [sb(f"sh_stage_place{i}", [P, 2, G], I32) for i in range(2)]
            stage_token = [sb(f"sh_stage_token{i}", [P, G], I32) for i in range(2)]

            def step(h, i):
                if past(h, 2):
                    pool.wait_ge(in_table[i], (h // 2 if isinstance(h, int) else h_half[0]) * (2 * G * 16))
                nc.gpsimd.tensor_copy(stage_place[i][:], keep["place"][:, :, bass.ds(h * G, G)]).then_inc(staged, 1)
                nc.gpsimd.tensor_copy(stage_token[i][:], keep["token"][:, bass.ds(h * G, G)]).then_inc(staged, 1)
                pool.wait_ge(staged, 2)
                pool.sem_clear(staged)
                for t in range(G):
                    for j in range(2):
                        nc.gpsimd.indirect_dma_start(
                            out=dram["table"], out_offset=bass.IndirectOffsetOnAxis(ap=stage_place[i][:, j, t:t + 1], axis=0),
                            in_=stage_token[i][:, t:t + 1], in_offset=None).then_inc(in_table[i], 16)

            S = NT // G
            h_half = [None]
            for h in range(2):
                step(h, h)
            with pool.Fori(1, S // 2) as hh_:
                h_half[0] = hh_
                for i in range(2):
                    step(2 * hh_ + i, i)
            for i in range(2):
                pool.wait_ge(in_table[i], (S // 2) * 2 * G * 16)

        @block.scalar
        def _(act):
            act.wait_ge(w_here, 64)
            nc.scalar.copy(w_part[0][:], w_in[:])
            nc.scalar.copy(wd_part[0][:], wd_in[:]).then_inc(w_high, 1)

            def high_x(b, i):
                if past(b, 2):
                    act.wait_ge(gu_in_psum, KF * b - KF)
                nc.scalar.copy(xh[i][:], keep["xT"][:, :, bass.ds(b * N, N)]).then_inc(xh_ready, 1)

            def tanh(b, f):
                act.wait_ge(gu_in_psum, KF * b + f + 1)
                if past(b, 1):
                    act.wait_ge(gs_ready, KF * b - KF + f + 1)
                nc.scalar.activation(th[f][:], ps_gu[f][0][:], ACT.Tanh, scale=0.5).then_inc(tanh_ready, 1)

            def high_h(b, i, f):
                act.wait_ge(hid_ready, KF * b + f + 1)
                if past(b, 2):
                    act.wait_ge(out_in_psum, (TB // 2) * (b - 1))
                nc.scalar.copy(hh[f][i][:], hid[f][:]).then_inc(hh_ready, 1)

            def step(b, i):
                if not isinstance(b, int) or b < B - 1:
                    high_x(b + 1, 1 - i)
                for f in range(KF):
                    tanh(b, f)
                for f in range(KF):
                    high_h(b, i, f)

            high_x(0, 0)
            step(0, 0)
            step(1, 1)
            with act.Fori(1, B // 2 - 1) as h:
                for i in range(2):
                    step(2 * h + i, i)
            step(B - 2, 0)
            step(B - 1, 1)

        @block.vector
        def _(dve):
            dve.wait_ge(w_high, 1)
            nc.vector.tensor_tensor(w_part[1][:], w_in[:], f32(w_part[0][:]), ALU.subtract)
            nc.vector.tensor_tensor(wd_part[1][:], wd_in[:], f32(wd_part[0][:]), ALU.subtract).then_inc(w_low, 1)

            def low_x(b, i):
                dve.wait_ge(xh_ready, b + 1)
                if past(b, 2):
                    dve.wait_ge(gu_in_psum, KF * b - KF)
                nc.vector.tensor_tensor(xl[i][:], keep["xT"][:, :, bass.ds(b * N, N)], f32(xh[i][:]),
                                        ALU.subtract).then_inc(xl_ready, 1)

            def hidden(b, f):
                dve.wait_ge(tanh_ready, KF * b + f + 1)
                nc.vector.scalar_tensor_tensor(out=gs[f][:], in0=th[f][:], scalar=1.0, in1=ps_gu[f][0][:],
                                               op0=ALU.add, op1=ALU.mult).then_inc(gs_ready, 1)
                dve.wait_ge(gs_ready, KF * b + f + 1)
                if past(b, 1):
                    dve.wait_ge(hh_ready, KF * b - KF + f + 1)
                    dve.wait_ge(hl_ready, KF * b - KF + f + 1)
                nc.vector.scalar_tensor_tensor(out=hid[f][:], in0=gs[f][:], scalar=0.5, in1=ps_gu[f][1][:],
                                               op0=ALU.mult, op1=ALU.mult).then_inc(hid_ready, 1)

            def low_h(b, i, f):
                dve.wait_ge(hh_ready, KF * b + f + 1)
                nc.vector.tensor_tensor(hl[f][i][:], hid[f][:], f32(hh[f][i][:]), ALU.subtract).then_inc(hl_ready, 1)

            def add_bias(b, hb, i):
                dve.wait_ge(x_here[i], 16 * hb + 16)
                nc.vector.tensor_tensor(xb[i][:], x_in[i][:], bias[:].unsqueeze(1).broadcast_to([P, TB, D]),
                                        ALU.add).then_inc(xb_ready, 1)

            def take_out(b, hb, i):
                if past(b, 2):
                    dve.wait_ge(part_stored[i], 16 * hb)
                dve.wait_ge(xb_ready, b + 1)
                for o in range(TB // 2):
                    dve.wait_ge(out_in_psum, (TB // 2) * b + o + 1)
                    nc.vector.tensor_tensor(part[i][:, 2 * o:2 * o + 2, :], ps_out[o][:],
                                            xb[i][:, 2 * o:2 * o + 2, :], ALU.add).then_inc(part_ready, 1)

            def step(b, hb, i, first=False, end=False):
                if not end:
                    low_x(b + 1, 1 - i)
                for f in range(KF):
                    hidden(b, f)
                if not first:
                    take_out(b - 1, hb if i else hb - 1, 1 - i)
                add_bias(b, hb, i)
                for f in range(KF):
                    low_h(b, i, f)

            low_x(0, 0)
            step(0, 0, 0, first=True)
            step(1, 0, 1)
            step(2, 1, 0)
            step(3, 1, 1)
            with dve.Fori(2, B // 2 - 1) as h:
                for i in range(2):
                    step(2 * h + i, h, i)
            step(B - 2, B // 2 - 1, 0)
            step(B - 1, B // 2 - 1, 1, end=True)
            take_out(B - 1, B // 2 - 1, 1)

        @block.tensor
        def _(pe):
            pe.wait_ge(w_low, 1)

            def gate_up(b, i):
                pe.wait_ge(xl_ready, b + 1)
                for f in range(KF):
                    if past(b, 1):
                        pe.wait_ge(hid_ready, KF * b - KF + f + 1)
                    for g in range(2):
                        last = exact_products(
                            nc, ps_gu[f][g][:],
                            [[w_part[x][:, k, g, f * P:(f + 1) * P] for x in range(2)] for k in range(KD)],
                            [[(xh, xl)[x][i][:, k, :] for x in range(2)] for k in range(KD)])
                    last.then_inc(gu_in_psum, 1)

            def down(b, i):
                pe.wait_ge(hl_ready, KF * b + KF)
                for o in range(TB // 2):
                    if past(b, 1):
                        pe.wait_ge(part_ready, (TB // 2) * (b - 1) + o + 1)
                    for t in (2 * o, 2 * o + 1):
                        last = exact_products(
                            nc, ps_out[o][:, t % 2, :],
                            [[(hh, hl)[x][f][i][:, t * P:(t + 1) * P] for x in range(2)] for f in range(KF)],
                            [[wd_part[x][:, f, :] for x in range(2)] for f in range(KF)])
                    last.then_inc(out_in_psum, 1)

            def step(b, i):
                if not (isinstance(b, int) and b >= B):
                    gate_up(b, i)
                if past(b, 1):
                    down(b - 1, 1 - i)

            steps(pe, step, B, peeled=2, trailing=1)


def phase_experts(nc, sh, dram, keep):
    D, KD, E, F, ST = sh.D, sh.KD, sh.E, sh.F, sh.SLOT_TILES
    PAIRS = ST // 2
    U = 4
    WC = 4
    with ExitStack() as ctx:
        def sb(name, shape, dt=F32):
            return ctx.enter_context(nc.sbuf_tensor(f"ex_{name}", shape, dt))

        def ps(name, shape):
            return ctx.enter_context(nc.psum_tensor(f"ex_{name}", shape, F32))

        def sem(name):
            return ctx.enter_context(nc.semaphore(f"ex_{name}"))

        w_in = [sb(f"w_in{i}", [P, WC, KD, 2, F]) for i in range(2)]
        wd_in = [sb(f"wd_in{i}", [P, WC, D]) for i in range(2)]
        w_part = [sb(f"w_part{x}", [P, E, KD, 2 * F], F32R) for x in range(2)]
        wd_part = [sb(f"wd_part{x}", [P, E, D], F32R) for x in range(2)]
        w_rows = [w[:].rearrange("p e k f -> p (e k) f") for w in w_part]
        qkv_in = sb("qkv_in", [P, KD, 3 * D])
        proj_in = sb("proj_in", [P, KD, D])
        table = sb("table", [P, ST], I32)
        stage = [sb(f"stage{i}", [P, 2], I32) for i in range(U)]
        xg = [sb(f"xg{i}", [P, 2, D]) for i in range(U)]
        xh = [sb(f"xh{i}", [P, 2 * KD, P], F32R) for i in range(2)]
        xl = [sb(f"xl{i}", [P, 2 * KD, P], F32R) for i in range(2)]
        th = [sb(f"tanh{i}", [P, 2, F]) for i in range(2)]
        gs = [sb(f"gs{i}", [P, 2, F]) for i in range(2)]
        hid = [sb(f"hid{i}", [P, 2, F]) for i in range(2)]
        hh = [sb(f"hh{i}", [P, 2, P], F32R) for i in range(2)]
        hl = [sb(f"hl{i}", [P, 2, P], F32R) for i in range(2)]
        y = [sb(f"y{i}", [P, 2, D]) for i in range(2)]
        ps_x = [ps(f"ps_x{i}", [P, 2 * KD, P]) for i in range(2)]
        ps_gu = [ps(f"ps_gu{i}", [P, 2, 2 * F]) for i in range(2)]
        ps_h = [ps(f"ps_h{i}", [P, 4, P]) for i in range(2)]
        ps_y = [ps(f"ps_y{i}", [P, 2, D]) for i in range(2)]

        w_here = [sem(f"w_here{i}") for i in range(2)]
        w_high, w_low = sem("w_high"), sem("w_low")
        at_here, at_high = sem("at_here"), sem("at_high")
        table_here = sem("table_here")
        staged = sem("staged")
        xg_here = [sem(f"xg_here{i}") for i in range(U)]
        x_in_psum, xh_ready, xl_ready = sem("x_in_psum"), sem("xh_ready"), sem("xl_ready")
        gu_in_psum, tanh_ready, gs_ready, hid_ready = (
            sem("gu_in_psum"), sem("tanh_ready"), sem("gs_ready"), sem("hid_ready"))
        h_in_psum, hh_ready, hl_ready = sem("h_in_psum"), sem("hh_ready"), sem("hl_ready")
        y_in_psum, y_ready = sem("y_in_psum"), sem("y_ready")
        y_stored = [sem(f"y_stored{i}") for i in range(2)]
        CHUNKS = E // WC
        block = ctx.enter_context(nc.Block())

        @block.sync
        def _(sp):
            sp.dma_start(table[:], dram["table"].rearrange("(p j) o -> p (j o)", p=P)).then_inc(table_here, 16)
            for c in range(CHUNKS):
                i, experts = c % 2, slice(c * WC, (c + 1) * WC)
                if c >= 2:
                    sp.wait_ge(w_low, c - 1)
                for e in range(WC):
                    for g, w in enumerate((dram["Wg"], dram["Wu"])):
                        sp.dma_start(w_in[i][:, e, :, g, :],
                                     w[c * WC + e].rearrange("(k p) f -> p k f", p=P)).then_inc(w_here[i], 16)
                sp.dma_start(wd_in[i][:], dram["Wd"][experts].rearrange("e f d -> f e d")).then_inc(w_here[i], 16)

            sp.dma_start(qkv_in[:], dram["qkv_wT"].rearrange("(k p) d -> p k d", p=P)).then_inc(at_here, 16)
            sp.dma_start(proj_in[:], dram["proj_wT"].rearrange("(k p) d -> p k d", p=P)).then_inc(at_here, 16)

            def step(p, i):
                i = i % 2
                at = p * (2 * P) if isinstance(p, int) else sp.snap(p * (2 * P))
                ready = p + 1 if isinstance(p, int) else sp.snap(p + 1)
                sp.wait_ge(y_ready, ready)
                sp.dma_start(dram["y"][bass.ds(at, 2 * P), :].rearrange("(u p) d -> p u d", p=P),
                             y[i][:]).then_inc(y_stored[i], 16)

            steps(sp, step, PAIRS, unroll=2, peeled=0)
            for i in range(2):
                sp.wait_ge(y_stored[i], 16 * (PAIRS // 2))

        @block.gpsimd
        def _(pool):
            pool.wait_ge(table_here, 16)

            def step(p, i):
                if past(p, U):
                    pool.wait_ge(x_in_psum, p - (U - 1))
                nc.gpsimd.tensor_copy(stage[i][:], table[:, bass.ds(2 * p, 2)]).then_inc(staged, 1)
                pool.wait_ge(staged, 1)
                pool.sem_clear(staged)
                for u in range(2):
                    nc.gpsimd.indirect_dma_start(
                        out=xg[i][:, u, :], out_offset=None, in_=dram["xn"],
                        in_offset=bass.IndirectOffsetOnAxis(ap=stage[i][:, u:u + 1], axis=0)).then_inc(xg_here[i], 16)

            steps(pool, step, PAIRS, unroll=U)

        @block.scalar
        def _(act):
            for c in range(CHUNKS):
                i, experts = c % 2, slice(c * WC, (c + 1) * WC)
                act.wait_ge(w_here[i], (2 * WC + 1) * 16 * (c // 2 + 1))
                nc.scalar.copy(w_part[0][:, experts].rearrange("p e k f -> p (e k f)"),
                               w_in[i][:].rearrange("p e k g f -> p (e k g f)"))
                nc.scalar.copy(wd_part[0][:, experts], wd_in[i][:]).then_inc(w_high, 1)

            def step(p, i):
                i = i % 2
                if not (isinstance(p, int) and p >= PAIRS):
                    act.wait_ge(x_in_psum, p + 1)
                    if past(p, 2):
                        act.wait_ge(gu_in_psum, p - 1)
                    nc.scalar.copy(xh[i][:], ps_x[i][:]).then_inc(xh_ready, 1)
                if past(p, 1) and not (isinstance(p, int) and p - 1 >= PAIRS):
                    act.wait_ge(gu_in_psum, p)
                    if past(p, 3):
                        act.wait_ge(gs_ready, p - 2)
                    nc.scalar.activation(th[1 - i][:], ps_gu[1 - i][:, :, 0:F], ACT.Tanh, scale=0.5).then_inc(tanh_ready, 1)
                if past(p, 2) and not (isinstance(p, int) and p - 2 >= PAIRS):
                    act.wait_ge(h_in_psum, p - 1)
                    if past(p, 4):
                        act.wait_ge(y_in_psum, p - 3)
                    nc.scalar.copy(hh[i][:], ps_h[i][:, 0:2, :]).then_inc(hh_ready, 1)
                if past(p, 3):
                    act.wait_ge(y_in_psum, p - 2)
                    if past(p, 5):
                        act.wait_ge(y_stored[1 - i], stored(p))
                    nc.scalar.copy(y[1 - i][:], ps_y[1 - i][:]).then_inc(y_ready, 1)

            half = [None]

            def stored(p):
                if isinstance(p, int):
                    return 16 * ((p - 3) // 2)
                h, i = half[0]
                return (2 * h + (i - 3) // 2) * 16

            for p in range(8):
                step(p, p % 4)
            act.wait_ge(at_here, 32)
            nc.scalar.copy(keep["qkv_part"][0][:], qkv_in[:])
            nc.scalar.copy(keep["proj_part"][0][:], proj_in[:]).then_inc(at_high, 1)
            with act.Fori(2, PAIRS // 4) as h:
                for i in range(4):
                    half[0] = (h, i)
                    step(4 * h + i, i)
            for p in range(PAIRS, PAIRS + 3):
                step(p, p % 4)

        @block.vector
        def _(dve):
            for c in range(CHUNKS):
                i, experts = c % 2, slice(c * WC, (c + 1) * WC)
                dve.wait_ge(w_high, c + 1)
                nc.vector.tensor_tensor(w_part[1][:, experts].rearrange("p e k f -> p (e k f)"),
                                        w_in[i][:].rearrange("p e k g f -> p (e k g f)"),
                                        f32(w_part[0][:, experts]).rearrange("p e k f -> p (e k f)"), ALU.subtract)
                nc.vector.tensor_tensor(wd_part[1][:, experts], wd_in[i][:], f32(wd_part[0][:, experts]),
                                        ALU.subtract).then_inc(w_low, 1)

            def step(p, i):
                i = i % 2
                if not (isinstance(p, int) and p >= PAIRS):
                    dve.wait_ge(xh_ready, p + 1)
                    nc.vector.tensor_tensor(xl[i][:], ps_x[i][:], f32(xh[i][:]), ALU.subtract).then_inc(xl_ready, 1)
                if past(p, 1) and not (isinstance(p, int) and p - 1 >= PAIRS):
                    dve.wait_ge(tanh_ready, p)
                    nc.vector.scalar_tensor_tensor(out=gs[1 - i][:], in0=th[1 - i][:], scalar=1.0,
                                                   in1=ps_gu[1 - i][:, :, 0:F], op0=ALU.add, op1=ALU.mult).then_inc(gs_ready, 1)
                if past(p, 2) and not (isinstance(p, int) and p - 2 >= PAIRS):
                    dve.wait_ge(hh_ready, p - 1)
                    nc.vector.tensor_tensor(hl[i][:], ps_h[i][:, 0:2, :], f32(hh[i][:]), ALU.subtract).then_inc(hl_ready, 1)
                if past(p, 1) and not (isinstance(p, int) and p - 1 >= PAIRS):
                    dve.wait_ge(gs_ready, p)
                    if past(p, 3):
                        dve.wait_ge(h_in_psum, p - 2)
                    nc.vector.scalar_tensor_tensor(out=hid[1 - i][:], in0=gs[1 - i][:], scalar=0.5,
                                                   in1=ps_gu[1 - i][:, :, F:2 * F], op0=ALU.mult, op1=ALU.mult).then_inc(hid_ready, 1)

            steps(dve, step, PAIRS, unroll=4, peeled=4, trailing=2)
            dve.wait_ge(at_high, 1)
            for part, whole in ((keep["qkv_part"], qkv_in), (keep["proj_part"], proj_in)):
                nc.vector.tensor_tensor(part[1][:], whole[:], f32(part[0][:]), ALU.subtract)

        @block.tensor
        def _(pe):
            def experts_of(p):
                word = pe.value_load(keep["experts"][0:1, bass.ds(p, 1)], min_val=0, max_val=E ** 4 - 1)
                return [pe.snap((word // E ** n) % E, min_val=0, max_val=E - 1) for n in range(4)]

            def transpose_x(p, i):
                pe.wait_ge(xg_here[i], gathered(p))
                if past(p, 2):
                    pe.wait_ge(xl_ready, p - 1)
                for u in range(2):
                    for k in range(KD):
                        last = nc.tensor.transpose(ps_x[i % 2][:, u * KD + k, :], xg[i][:, u, k * P:(k + 1) * P],
                                                   keep["ident"][:])
                last.then_inc(x_in_psum, 1)

            def gate_up(p, i, experts):
                pe.wait_ge(xl_ready, p + 1)
                if past(p, 2):
                    pe.wait_ge(hid_ready, p - 1)
                for u in range(2):
                    e = experts[u]
                    last = exact_products(
                        nc, ps_gu[i][:, u, :],
                        [[(xh, xl)[x][i][:, u * KD + k, :] for x in range(2)] for k in range(KD)],
                        [[w_rows[x][:, bass.ds(e * KD + k, 1), :] for x in range(2)] for k in range(KD)])
                last.then_inc(gu_in_psum, 1)

            def transpose_h(p, i):
                pe.wait_ge(hid_ready, p + 1)
                if past(p, 2):
                    pe.wait_ge(hl_ready, p - 1)
                for u in range(2):
                    last = nc.tensor.transpose(ps_h[i][:, u, :], hid[i][:, u, :], keep["ident"][:])
                last.then_inc(h_in_psum, 1)

            def down(p, i, experts):
                pe.wait_ge(hl_ready, p + 1)
                if past(p, 2):
                    pe.wait_ge(y_ready, p - 1)
                for u in range(2):
                    e = experts[u]
                    last = exact_products(nc, ps_y[i][:, u, :], [[(hh, hl)[x][i][:, u, :] for x in range(2)]],
                                          [[wd_part[x][:, bass.ds(e, 1), :] for x in range(2)]])
                last.then_inc(y_in_psum, 1)

            group = [None]

            def gathered(p):
                return 32 * (p // U + 1) if isinstance(p, int) else 32 * group[0] + 32

            def step(p, i):
                inside = not isinstance(p, int) or p < PAIRS
                experts = experts_of(p)
                if inside:
                    transpose_x(p, i)
                i = i % 2
                if past(p, 1) and not (isinstance(p, int) and p - 1 >= PAIRS):
                    gate_up(p - 1, 1 - i, experts[0:2])
                if past(p, 2) and not (isinstance(p, int) and p - 2 >= PAIRS):
                    transpose_h(p - 2, i)
                if past(p, 3):
                    down(p - 3, 1 - i, experts[2:4])

            for p in range(U):
                if p == 1:
                    pe.wait_ge(w_low, CHUNKS)
                step(p, p)
            with pe.Fori(1, PAIRS // U) as h:
                group[0] = h
                for i in range(U):
                    step(U * h + i, i)
            for p in range(PAIRS, PAIRS + 3):
                step(p, p % U)


def phase_attention(nc, sh, dram, keep):
    B, N, D, KD, TB, H, HD, M, BS = sh.B, sh.N, sh.D, sh.KD, sh.TB, sh.H, sh.HD, sh.M, sh.BS
    G = 4
    Q = H // G
    HG = P // HD
    SB = Q * TB
    QK0 = M
    TOP0 = M + 4 * HD
    ROWS = TOP0 + 2
    WORK = {1: ("qk", 0), 3: ("qk", 1), 4: ("turn", 0), 5: ("select", 0), 6: ("turn", 1), 7: ("qk", 2),
            8: ("final", 0), 9: ("qk", 3), 10: ("final", 1), 11: ("select", 1), 12: ("v", 0), 13: ("v", 1)}
    BANK = {work: i % 2 for i, work in enumerate(WORK.values())}
    AHEAD = ("qk", "select", "v")
    with ExitStack() as ctx:
        def sb(name, shape, dt=F32):
            return ctx.enter_context(nc.sbuf_tensor(f"at_{name}", shape, dt))

        def ps(name, shape):
            return ctx.enter_context(nc.psum_tensor(f"at_{name}", shape, F32))

        def sem(name):
            return ctx.enter_context(nc.semaphore(f"at_{name}"))

        stack = [[sb(f"stack{s}{q}", [ROWS, G, N], F32R) for q in range(Q)] for s in range(2)]
        pt = [sb(f"pt{t}", [P, G, N]) for t in range(TB)]
        w_part, wp_part = keep["qkv_part"], keep["proj_part"]
        v_raw = sb("v_raw", [P, TB, H, HD])
        vx = sb("vx", [P, TB, H, 2 * HD])
        ones = sb("ones", [P, TB, G, HD])
        x_in = sb("x_in", [P, KD, N])
        xh, xl = sb("xh", [P, KD, N], F32R), sb("xl", [P, KD, N], F32R)
        qk_part = [[sb(f"qk_part{s}{x}", [P, N], F32R) for x in range(2)] for s in range(2)]
        qk_sum = [[sb(f"qk_sum{s}{g}", [P, M]) for g in range(KD)] for s in range(2)]
        own_head = sb("own_head", [P, HG])
        k_own = sb("k_own", [P, HG, M])
        c_top = sb("c_top", [M, HG])
        kept = sb("kept", [M, HG, M])
        kept2 = sb("kept2", [M, HG, M])
        eye = sb("eye", [M, M])
        mask = [sb(f"mask{g}", [M, HG, M]) for g in range(KD)]
        top = [sb(f"top{i}", [P, G * TB]) for i in range(2)]
        top_part = [[sb(f"top_part{i}{x}", [G * TB, P], F32R) for x in range(2)] for i in range(2)]
        o_unit = sb("o_unit", [P, N])
        rec = sb("rec", [P, TB, G])
        on = sb("on", [P, TB, D])
        on_part = [sb(f"on_part{x}", [P, KD, N], F32R) for x in range(2)]
        part = sb("part", [P, TB, D])
        yg = [sb(f"yg{j}", [P, TB, D]) for j in range(2)]
        stage = sb("stage", [P, 2, TB], I32)
        ps_s = [ps(f"ps_s{i}", [P, N]) for i in range(2)]
        ps_st = [ps(f"ps_st{i}", [P, N]) for i in range(2)]
        ps_pv = ps("ps_pv", [P, N])
        ps_m = ps("ps_m", [P, TB, P])
        ps_work = [ps(f"ps_work{i}", [P, N]) for i in range(2)]

        consts, consts2, const_rows = sem("consts"), sem("consts2"), sem("const_rows")
        x_here, xh_ready, xl_ready = sem("x_here"), sem("xh_ready"), sem("xl_ready")
        qk_in_psum, qk_high, qk_taken = sem("qk_in_psum"), sem("qk_high"), sem("qk_taken")
        qk_out = [sem(f"qk_out{g}") for g in range(KD)]
        k_own_ready, c_in_psum, select_order, mask_ready = (
            sem("k_own_ready"), sem("c_in_psum"), sem("select_order"), sem("mask_ready"))
        stack_here = [sem(f"stack_here{q}") for q in range(Q)]
        mask_rows = sem("mask_rows")
        s_in_psum, s_max = sem("s_in_psum"), sem("s_max")
        top_in_psum, top_high, top_low = sem("top_in_psum"), sem("top_high"), sem("top_low")
        top_here = [sem(f"top_here{i}") for i in range(2)]
        st_in_psum, exp_ready = sem("st_in_psum"), sem("exp_ready")
        v_in_psum, v_ready, v_quads = sem("v_in_psum"), sem("v_ready"), sem("v_quads")
        pv_in_psum, pv_ready = sem("pv_in_psum"), sem("pv_ready")
        ot_in_psum, rec_ready, on_ready = sem("ot_in_psum"), sem("rec_ready"), sem("on_ready")
        on_in_psum, on_high, on_low = sem("on_in_psum"), sem("on_high"), sem("on_low")
        fin_in_psum, fin_ready = sem("fin_in_psum"), sem("fin_ready")
        staged, y_here, added = sem("staged"), sem("y_here"), sem("added")
        part_here, out_stored = sem("part_here"), sem("out_stored")

        tokens = lambda t: t.rearrange("(b t p) d -> b p t d", p=P, t=TB)
        part_tok = tokens(dram["part"])
        out_tok = dram["out"].rearrange("b (t p) d -> b p t d", p=P)
        one = lambda ap: ap.rearrange("o p t d -> (o p) t d")
        block = ctx.enter_context(nc.Block())

        def batches(engine, body):
            body(0, first=True)
            with engine.Fori(1, B - 2) as b:
                body(b)
            body(B - 2)
            body(B - 1, last=True)

        def work_of(step, first, last):
            name, which = WORK.get(step, (None, None))
            if name is None or (last and name in AHEAD) or (first and name not in AHEAD):
                return None, None
            return name, which

        @block.sync
        def _(sp):
            def val(x):
                return x if isinstance(x, int) else sp.snap(x)

            def load_x(b):
                at, used = val(b), val(b)
                if past(b, 1):
                    sp.wait_ge(xl_ready, used)
                sp.dma_start(x_in[:], one(dram["xT"][bass.ds(at, 1)])).then_inc(x_here, 16)

            def store_qk(b, j):
                g, s = j // 2, j % 2
                at, ready = val(b), val(2 * KD * b + j + 1)
                sp.wait_ge(qk_taken, ready)
                for x in range(2):
                    sp.dma_start(dram["qkT"][bass.ds(at, 1), s, g, :, x, :].rearrange("o p n -> (o p) n"),
                                 f32(qk_part[s][x][:])).then_inc(qk_out[g], 16)
                    if s == 1:
                        sp.dma_start(dram["qkT"][bass.ds(at, 1), 2, g, :, 1 - x, :].rearrange("o p n -> (o p) n"),
                                     f32(qk_part[s][x][:])).then_inc(qk_out[g], 16)

            def load_stack(b, q):
                at, out = val(b), val(96 * b + 96)
                sp.wait_ge(qk_out[q // 2], out)
                lanes = slice((q % 2) * G * HD, (q % 2 + 1) * G * HD)
                for s in range(2):
                    for half in range(2):
                        row = QK0 + half * 2 * HD
                        src = dram["qkT"][bass.ds(at, 1), s + s * half, q // 2, lanes]
                        sp.dma_start(f32(stack[s][q][row:row + 2 * HD, :, :]),
                                     src.rearrange("o (h d) x n -> (o d x) h n", d=HD)).then_inc(stack_here[q], 16)

            def top_rows(b, q):
                ready = val(Q * b + q + 1)
                sp.wait_ge(top_low, ready)
                for x in range(2):
                    sp.dma_start(f32(stack[0][q][TOP0 + x:TOP0 + x + 1, :, :]).rearrange("o g n -> o (g n)"),
                                 f32(top_part[q % 2][x][:])).then_inc(top_here[q % 2], 16)

            def store_out(b):
                at, ready = val(b), val(2 * b + 2)
                sp.wait_ge(fin_ready, ready)
                sp.dma_start(one(out_tok[bass.ds(at, 1)]), part[:]).then_inc(out_stored, 16)

            def load_part(b):
                at, stored = val(b), val(16 * b)
                if past(b, 1):
                    sp.wait_ge(out_stored, stored)
                sp.dma_start(part[:], one(part_tok[bass.ds(at, 1)])).then_inc(part_here, 16)

            load_x(0)
            sp.wait_ge(consts, 1)
            for q in range(Q):
                sp.dma_start(f32(stack[1][q][TOP0:ROWS, :, :]),
                             part[0:2, 0:2, :].rearrange("p t d -> p (t d)").unsqueeze(1)
                             .broadcast_to([2, G, N])).then_inc(const_rows, 16)
            for j in range(2 * KD):
                store_qk(0, j)
            for q in range(Q):
                load_stack(0, q)
            sp.wait_ge(const_rows, 16 * Q)
            load_part(0)
            top_rows(0, 0)

            load_x(1)

            def body(b, first=False, last=False):
                top_rows(b, 1)
                if not first:
                    load_stack(b, 3)
                if not last:
                    store_qk(b + 1, 0)
                    store_qk(b + 1, 1)
                top_rows(b, 2)
                if not last:
                    load_stack(b + 1, 0)
                    store_qk(b + 1, 2)
                top_rows(b, 3)
                if not last:
                    load_stack(b + 1, 1)
                    store_qk(b + 1, 3)
                if not first:
                    store_out(b - 1)
                if not isinstance(b, int) or b + 2 < B:
                    load_x(b + 2)
                if not first:
                    load_part(b)
                if not last:
                    top_rows(b + 1, 0)
                    load_stack(b + 1, 2)

            batches(sp, body)
            store_out(B - 1)
            sp.wait_ge(out_stored, 16 * B)

        @block.gpsimd
        def _(pool):
            nc.gpsimd.memset(part[0:2, 0:2, :], -1.0).then_inc(consts, 1)
            nc.gpsimd.memset(vx[:], 0.0).then_inc(consts2, 1)
            for t in (o_unit[0:M, :], eye[:], own_head[:]):
                nc.gpsimd.memset(t, 1.0).then_inc(consts2, 1)
            pool.wait_ge(consts2, 4)
            nc.gpsimd.memset(vx[:, :, :, HD:HD + 1], 1.0).then_inc(consts2, 1)
            for t, pattern in ((o_unit[0:M, :], [[1, M], [0, BS]]), (eye[:], [[1, M]])):
                nc.gpsimd.affine_select(out=t, in_=t, compare_op=ALU.is_equal, fill=0.0, base=0, pattern=pattern,
                                        channel_multiplier=-1).then_inc(consts2, 1)
            nc.gpsimd.affine_select(out=own_head[:], in_=own_head[:], compare_op=ALU.is_ge, fill=0.0, base=0,
                                    pattern=[[-HD, HG]], channel_multiplier=1).then_inc(consts2, 1)
            pool.wait_ge(consts2, 8)
            nc.gpsimd.affine_select(out=own_head[:], in_=own_head[:], compare_op=ALU.is_gt, fill=0.0, base=HD,
                                    pattern=[[HD, HG]], channel_multiplier=-1).then_inc(consts2, 1)
            nc.gpsimd.memset(ones[:], 1.0).then_inc(consts2, 1)

            def low_x(b):
                pool.wait_ge(xh_ready, b + 1)
                nc.gpsimd.tensor_tensor(xl[:], x_in[:], f32(xh[:]), ALU.subtract).then_inc(xl_ready, 1)

            def v_quad(b, q):
                pool.wait_ge(v_ready, 2 * b + 2)
                if past(b, 1):
                    pool.wait_ge(pv_in_psum, SB * (b - 1) + TB * (q + 1))
                nc.gpsimd.tensor_tensor(vx[:, :, G * q:G * (q + 1), 0:HD], v_raw[:, :, G * q:G * (q + 1), :],
                                        ones[:], ALU.mult).then_inc(v_quads, 1)

            def mask_quad(b, q):
                pool.wait_ge(mask_ready, KD * b + q // 2 + 1)
                if past(b, 1):
                    pool.wait_ge(st_in_psum, G * (SB * (b - 1) + TB * (q + 1)))
                heads = mask[q // 2][:, (q % 2) * G:(q % 2 + 1) * G, :].rearrange("m h n -> m (h n)")
                heads = heads.unsqueeze(2).broadcast_to([M, G * M, BS])
                nc.gpsimd.tensor_tensor(stack[1][q][0:M, :, :].rearrange("m h (n c) -> m (h n) c", c=BS),
                                        heads, heads, ALU.add).then_inc(mask_rows, 1)

            def gather_y(b):
                if past(b, 1):
                    pool.wait_ge(added, 4 * b)
                nc.gpsimd.tensor_copy(stage[:], keep["slot"][:, :, bass.ds(TB * b, TB)]).then_inc(staged, 1)
                pool.wait_ge(staged, 1)
                pool.sem_clear(staged)
                for j in range(2):
                    for t in range(TB):
                        nc.gpsimd.indirect_dma_start(
                            out=yg[j][:, t, :], out_offset=None, in_=dram["y"],
                            in_offset=bass.IndirectOffsetOnAxis(ap=stage[:, j, t:t + 1], axis=0)).then_inc(y_here, 16)

            def add_y(b):
                pool.wait_ge(y_here, 2 * TB * 16 * (b + 1))
                for j in range(2):
                    nc.gpsimd.tensor_tensor(
                        yg[j][:], yg[j][:],
                        keep["weight"][:, j, bass.ds(TB * b, TB)].unsqueeze(2).broadcast_to([P, TB, D]),
                        ALU.mult).then_inc(added, 1)
                pool.wait_ge(part_here, 16 * b + 16)
                for j in range(2):
                    pool.wait_ge(added, 4 * b + 2 + j)
                    nc.gpsimd.tensor_tensor(part[:], part[:], yg[j][:], ALU.add).then_inc(added, 1)

            low_x(0)
            for q in range(Q):
                mask_quad(0, q)
            pool.wait_ge(consts2, 10)
            for q in range(Q - 1):
                v_quad(0, q)

            def body(b, first=False, last=False):
                if not last:
                    low_x(b + 1)
                v_quad(b, Q - 1)
                if not first:
                    mask_quad(b, Q - 1)
                    add_y(b - 1)
                if not last:
                    mask_quad(b + 1, 0)
                gather_y(b)
                if not last:
                    mask_quad(b + 1, 1)
                    mask_quad(b + 1, 2)
                    for q in range(Q - 1):
                        v_quad(b + 1, q)

            batches(pool, body)
            add_y(B - 1)

        @block.scalar
        def _(act):
            act.wait_ge(consts2, 9)
            for q in range(Q):
                last = nc.scalar.copy(stack[0][q][0:M, :, :], o_unit[0:M, :].unsqueeze(1).broadcast_to([M, G, N]))
            last.then_inc(consts, 1)

            def high_x(b):
                act.wait_ge(x_here, 16 * b + 16)
                if past(b, 1):
                    act.wait_ge(v_in_psum, 2 * b)
                nc.scalar.copy(xh[:], x_in[:]).then_inc(xh_ready, 1)

            def high_qk(b, j):
                g, s = j // 2, j % 2
                act.wait_ge(qk_in_psum, 2 * KD * b + j + 1)
                if g == 1:
                    act.wait_ge(qk_out[0], 96 * b + 96)
                elif past(b, 1):
                    act.wait_ge(qk_out[1], 96 * b)
                nc.scalar.copy(qk_part[s][0][:], ps_work[BANK['qk', j]][:]).then_inc(qk_high, 1)

            def take_v(b, o):
                act.wait_ge(v_in_psum, 2 * b + o + 1)
                if o == 0 and past(b, 1):
                    act.wait_ge(v_quads, Q * b)
                nc.scalar.copy(v_raw[:, 2 * o:2 * o + 2, :, :],
                               ps_work[BANK["v", o]][:].rearrange("p (t h d) -> p t h d", t=2, h=H)).then_inc(v_ready, 1)

            def high_on(b, c):
                act.wait_ge(on_in_psum, KD * b + c + 1)
                if past(b, 1):
                    act.wait_ge(fin_in_psum, 2 * b)
                nc.scalar.copy(on_part[0][:, c, :], ps_work[BANK['turn', c]][:]).then_inc(on_high, 1)

            def take_pv(u):
                act.wait_ge(pv_in_psum, TB * (u + 1))
                if past(u, 1):
                    act.wait_ge(ot_in_psum, u)
                nc.scalar.copy(o_unit[:], ps_pv[:]).then_inc(pv_ready, 1)

            def exp_head(n, t, g):
                act.wait_ge(st_in_psum, G * n + g + 1)
                if g == 0 and past(n, TB):
                    act.wait_ge(pv_in_psum, n - TB + 1)
                nc.scalar.activation(pt[t][:, g, :], ps_st[g % 2][:], ACT.Exp,
                                     scale=float(HD) ** -0.5).then_inc(exp_ready, 1)

            def work(b, name, which):
                if name == "qk":
                    high_qk(b + 1, which)
                elif name == "v":
                    take_v(b + 1, which)
                elif name == "turn":
                    high_on(b - 1, which)

            high_x(0)
            for j in range(2 * KD):
                high_qk(0, j)
            for o in range(2):
                take_v(0, o)

            def body(b, first=False, last=False):
                for i in range(SB):
                    q, t = i // TB, i % TB
                    n = SB * b + i
                    if i == 0 and not last:
                        high_x(b + 1)
                    exp_head(n, t, 0)
                    exp_head(n, t, 1)
                    work(b, *work_of(i - 1, first, last))
                    exp_head(n, t, 2)
                    exp_head(n, t, 3)
                    if t == 0 and past(n, 1):
                        take_pv(Q * b + q - 1)

            batches(act, body)
            take_pv(Q * B - 1)
            for c in range(KD):
                high_on(B - 1, c)

        @block.vector
        def _(dve):
            v = nc.vector
            dve.wait_ge(consts2, 9)

            def take_qk(b, j):
                g, s = j // 2, j % 2
                dve.wait_ge(qk_high, 2 * KD * b + j + 1)
                bank = ps_work[BANK["qk", j]]
                v.tensor_tensor(qk_part[s][1][:], bank[:], f32(qk_part[s][0][:]), ALU.subtract)
                v.tensor_reduce(qk_sum[s][g][:], bank[:].rearrange("p (m c) -> p m c", c=BS), AX,
                                ALU.add).then_inc(qk_taken, 1)
                if s == 1:
                    own_k(b, g)

            def own_k(b, g):
                dve.wait_ge(qk_taken, 2 * KD * b + 2 * g + 2)
                if past(b, 1) or g > 0:
                    dve.wait_ge(c_in_psum, KD * b + g)
                v.tensor_tensor(k_own[:], qk_sum[1][g][:].unsqueeze(1).broadcast_to([P, HG, M]),
                                own_head[:].unsqueeze(2).broadcast_to([P, HG, M]), ALU.mult).then_inc(k_own_ready, 1)

            def select(b, g):
                order = Order(dve, select_order, 3 * (KD * b + g))
                dve.wait_ge(c_in_psum, KD * b + g + 1)
                c = ps_work[BANK["select", g]][0:M, 0:HG * M].rearrange("m (h n) -> m h n", h=HG)
                order.done(v.tensor_reduce(c_top[:], c, AX, ALU.max))
                order.wait()
                order.done(v.tensor_tensor(kept[:], c, c_top[:].unsqueeze(2).broadcast_to([M, HG, M]), ALU.is_ge))
                order.wait()
                order.done(v.tensor_tensor(kept2[:], kept[:], eye[:].unsqueeze(1).broadcast_to([M, HG, M]), ALU.max))
                order.wait()
                if past(b, 1):
                    dve.wait_ge(mask_rows, Q * (b - 1) + 2 * g + 2)
                v.tensor_scalar(mask[g][:], kept2[:], -1.0, -MASKED / 2, ALU.add, ALU.mult).then_inc(mask_ready, 1)

            def maxes(u, i, g, tiles):
                for t in tiles:
                    dve.wait_ge(s_in_psum, G * TB * u + TB * g + t + 1)
                    if g == 0 and t == 0 and past(u, 2):
                        dve.wait_ge(top_in_psum, u - 1)
                    v.tensor_reduce(top[i][:, TB * g + t:TB * g + t + 1], ps_s[t % 2][:], AX, ALU.max).then_inc(s_max, 1)

            def take_top(b, q):
                u, i = Q * b + q, q % 2
                dve.wait_ge(top_in_psum, u + 1)
                if past(b, 1) or q >= 2:
                    dve.wait_ge(top_here[i], 32 * (2 * b + q // 2))
                v.tensor_copy(top_part[i][0][:], ps_m[0:G * TB, 0, :]).then_inc(top_high, 1)
                dve.wait_ge(top_high, u + 1)
                v.tensor_tensor(top_part[i][1][:], ps_m[0:G * TB, 0, :], f32(top_part[i][0][:]),
                                ALU.subtract).then_inc(top_low, 1)

            def take_o(b, q):
                u = Q * b + q
                dve.wait_ge(ot_in_psum, u + 1)
                o = ps_m[:].rearrange("p t (g c) -> p t g c", g=G)
                if past(u, 1):
                    dve.wait_ge(on_ready, u)
                v.reciprocal(rec[:], o[:, :, :, HD]).then_inc(rec_ready, 1)
                dve.wait_ge(rec_ready, u + 1)
                if q == 0 and past(b, 1):
                    dve.wait_ge(on_in_psum, KD * b)
                v.tensor_tensor(on[:, :, q * G * HD:(q + 1) * G * HD].rearrange("p t (g d) -> p t g d", g=G),
                                o[:, :, :, 0:HD], rec[:].unsqueeze(3).broadcast_to([P, TB, G, HD]),
                                ALU.mult).then_inc(on_ready, 1)

            def low_on(b, c):
                dve.wait_ge(on_high, KD * b + c + 1)
                v.tensor_tensor(on_part[1][:, c, :], ps_work[BANK["turn", c]][:], f32(on_part[0][:, c, :]),
                                ALU.subtract).then_inc(on_low, 1)

            def add_final(b, o):
                dve.wait_ge(added, 4 * (b + 1))
                dve.wait_ge(fin_in_psum, 2 * b + o + 1)
                rows = part[:, 2 * o:2 * o + 2, :].rearrange("p t d -> p (t d)")
                v.tensor_tensor(rows, ps_work[BANK["final", o]][:], rows, ALU.add).then_inc(fin_ready, 1)

            def work(b, name, which):
                if name == "qk":
                    take_qk(b + 1, which)
                elif name == "select":
                    select(b + 1, which)
                elif name == "turn":
                    low_on(b - 1, which)
                elif name == "final":
                    add_final(b - 1, which)

            for j in range(2 * KD):
                take_qk(0, j)
                if j % 2:
                    select(0, j // 2)
            for g in range(G):
                maxes(0, 0, g, range(TB))
            take_top(0, 0)
            for g in range(G):
                maxes(1, 1, g, range(TB))

            def body(b, first=False, last=False):
                for i in range(SB):
                    q, t = i // TB, i % TB
                    ahead = not (last and q >= 2)
                    if ahead:
                        maxes(Q * b + q + 2, q % 2, t, (0, 1))
                    work(b, *work_of(i - 1, first, last))
                    if ahead:
                        maxes(Q * b + q + 2, q % 2, t, (2, 3))
                    if t == 1 and not (last and q == Q - 1):
                        take_top(b if q < Q - 1 else b + 1, (q + 1) % Q)
                    if t == 3 and q:
                        take_o(b, q - 1)
                    elif t == 3 and not first:
                        take_o(b - 1, Q - 1)

            batches(dve, body)
            take_o(B - 1, Q - 1)
            for c in range(KD):
                low_on(B - 1, c)
            for o in range(2):
                add_final(B - 1, o)

        @block.tensor
        def _(pe):
            pe.wait_ge(consts, 2)
            pe.wait_ge(const_rows, 16 * Q)

            def qk(b, j):
                g, s = j // 2, j % 2
                if j == 0:
                    pe.wait_ge(xl_ready, b + 1)
                cols = slice(s * D + g * P, s * D + (g + 1) * P)
                exact_products(nc, ps_work[BANK["qk", j]][:],
                               [[w_part[x][:, k, cols] for x in range(2)] for k in range(KD)],
                               [[(xh, xl)[x][:, k, :] for x in range(2)] for k in range(KD)]).then_inc(qk_in_psum, 1)

            def block_scores(b, g):
                pe.wait_ge(k_own_ready, KD * b + g + 1)
                nc.tensor.matmul(ps_work[BANK["select", g]][0:M, 0:HG * M], qk_sum[0][g][:], k_own[:].rearrange("p h m -> p (h m)"),
                                 start=True, stop=True).then_inc(c_in_psum, 1)

            def values(b, o):
                for t in (2 * o, 2 * o + 1):
                    last = exact_products(
                        nc, ps_work[BANK["v", o]][:, (t % 2) * D:(t % 2 + 1) * D],
                        [[(xh, xl)[x][:, k, t * P:(t + 1) * P] for x in range(2)] for k in range(KD)],
                        [[w_part[x][:, k, 2 * D:3 * D] for x in range(2)] for k in range(KD)])
                last.then_inc(v_in_psum, 1)

            def turn(b, c):
                if c == 0:
                    pe.wait_ge(on_ready, Q * (b + 1))
                for t in range(TB):
                    last = nc.tensor.transpose(ps_work[BANK["turn", c]][:, t * P:(t + 1) * P], on[:, t, c * P:(c + 1) * P],
                                               keep["ident"][:])
                last.then_inc(on_in_psum, 1)

            def final(b, o):
                if o == 0:
                    pe.wait_ge(on_low, KD * (b + 1))
                for t in (2 * o, 2 * o + 1):
                    last = exact_products(
                        nc, ps_work[BANK["final", o]][:, (t % 2) * D:(t % 2 + 1) * D],
                        [[on_part[x][:, c, t * P:(t + 1) * P] for x in range(2)] for c in range(KD)],
                        [[wp_part[x][:, c, :] for x in range(2)] for c in range(KD)])
                last.then_inc(fin_in_psum, 1)

            def bank_taken(b, name, which):
                return {"qk": (qk_taken, 2 * KD * (b + 1) + which + 1), "select": (mask_ready, KD * (b + 1) + which + 1),
                        "turn": (on_low, KD * (b - 1) + which + 1), "final": (fin_ready, 2 * (b - 1) + which + 1),
                        "v": (v_ready, 2 * (b + 1) + which + 1)}[name]

            def work(b, i, first, last):
                name, which = work_of(i, first, last)
                if name is None:
                    return
                before = [j for j in range(i) if work_of(j, first, last)[0] and BANK[WORK[j]] == BANK[name, which]]
                if before:
                    pe.wait_ge(*bank_taken(b, *work_of(before[-1], first, last)))
                else:
                    pe.wait_ge(v_ready, 2 * b + BANK[name, which] + 1)
                if name == "qk":
                    qk(b + 1, which)
                elif name == "select":
                    block_scores(b + 1, which)
                elif name == "v":
                    values(b + 1, which)
                elif name == "turn":
                    turn(b - 1, which)
                elif name == "final":
                    final(b - 1, which)

            def s_tile(b, q, g, t, first=False):
                if g == 0 and t == 0:
                    pe.wait_ge(stack_here[q], 64 * b + 64)
                    pe.wait_ge(mask_rows, Q * b + q + 1)
                n = G * TB * (Q * b + q) + TB * g + t
                if past(n, 2):
                    pe.wait_ge(s_max, n - 1)
                nc.tensor.matmul(ps_s[t % 2][:], stack[0][q][0:TOP0, g, t * P:(t + 1) * P],
                                 stack[1][q][0:TOP0, g, :], start=True, stop=True).then_inc(s_in_psum, 1)

            def top_by_query(u, q, taken):
                pe.wait_ge(s_max, G * TB * (u + 1))
                if taken is not None:
                    pe.wait_ge(*taken)
                nc.tensor.transpose(ps_m[0:G * TB, 0, :], top[q % 2][:], keep["ident"][:]).then_inc(top_in_psum, 1)

            def o_by_token(u, taken):
                pe.wait_ge(pv_ready, u + 1)
                pe.wait_ge(*taken)
                for t in range(TB):
                    last = nc.tensor.transpose(ps_m[:, t, :], o_unit[:, t * P:(t + 1) * P], keep["ident"][:])
                last.then_inc(ot_in_psum, 1)

            def st_tile(b, q, t, g):
                m = G * (SB * b + TB * q + t) + g
                if t == 0 and g == 0:
                    pe.wait_ge(top_here[q % 2], 64 * b + 32 * (q // 2) + 32)
                if past(m, 2):
                    pe.wait_ge(exp_ready, m - 1)
                nc.tensor.matmul(ps_st[g % 2][:], stack[1][q][:, g, t * P:(t + 1) * P], stack[0][q][:, g, :],
                                 start=True, stop=True).then_inc(st_in_psum, 1)

            def pv(u, q, t):
                pe.wait_ge(exp_ready, G * (TB * u + t + 1))
                if t == 0:
                    pe.wait_ge(v_quads, u + 1)
                    if past(u, 1):
                        pe.wait_ge(pv_ready, u)
                for g in range(G):
                    last = nc.tensor.matmul(ps_pv[2 * HD * g:2 * HD * (g + 1), :], vx[:, t, G * q + g, :],
                                            pt[t][:, g, :], start=(t == 0), stop=(t == TB - 1))
                last.then_inc(pv_in_psum, 1)

            qk(0, 0)
            qk(0, 1)
            pe.wait_ge(qk_taken, 2)
            block_scores(0, 0)
            pe.wait_ge(mask_ready, 1)
            qk(0, 2)
            pe.wait_ge(qk_taken, 3)
            qk(0, 3)
            pe.wait_ge(qk_taken, 4)
            block_scores(0, 1)
            pe.wait_ge(mask_ready, 2)
            for o in range(2):
                values(0, o)
            for q in range(2):
                for g in range(G):
                    for t in range(TB):
                        s_tile(0, q, g, t)
                if q == 0:
                    top_by_query(0, 0, None)

            def body(b, first=False, last=False):
                for i in range(SB):
                    q, t = i // TB, i % TB
                    ahead = not (last and q >= 2)
                    u = Q * b + q

                    def s_ahead(tile):
                        if ahead:
                            s_tile(b if q < 2 else b + 1, (q + 2) % Q, t, tile)

                    st_tile(b, q, t, 0)
                    s_ahead(0)
                    st_tile(b, q, t, 1)
                    s_ahead(1)
                    if t:
                        pv(u, q, t - 1)
                    elif past(u, 1):
                        pv(u - 1, (q - 1) % Q, TB - 1)
                    st_tile(b, q, t, 2)
                    s_ahead(2)
                    st_tile(b, q, t, 3)
                    s_ahead(3)
                    work(b, i, first, last)
                    if t == 0 and not (last and q == Q - 1):
                        top_by_query(u + 1, (q + 1) % Q, (on_ready, u - 1) if past(u, 2) else (top_low, u + 1))
                    if t == 2 and past(u, 1):
                        o_by_token(u - 1, (on_ready, u - 1) if last and q == Q - 1 else (top_low, u + 2))

            batches(pe, body)
            pv(Q * B - 1, Q - 1, TB - 1)
            o_by_token(Q * B - 1, (on_ready, Q * B - 1))
            for c in range(KD):
                pe.wait_ge(*((on_low, KD * (B - 1) + 1) if c else (fin_ready, 2 * (B - 1))))
                turn(B - 1, c)
            for o in range(2):
                pe.wait_ge(*((fin_ready, 2 * (B - 1) + 1) if o else (on_low, KD * B)))
                final(B - 1, o)


def build(nc, x, qkv_wT, proj_wT, proj_b, Wr, Wg, Wu, Wd, Sg, Su, Sd, out, phases=9):
    sh = Shapes(x, qkv_wT, Wr, Wg, Sg)
    dram = dict(x=x, qkv_wT=qkv_wT, proj_wT=proj_wT, proj_b=proj_b, Wr=Wr, Wg=Wg, Wu=Wu, Wd=Wd, Sg=Sg, Su=Su,
                Sd=Sd, out=out)

    def scratch(name, shape, dt=F32):
        dram[name] = nc.dram_tensor(f"scratch_{name}", list(shape), dt, kind="Internal").ap()

    slots = sh.SLOT_TILES * P
    scratch("xn", [sh.T, sh.D])
    scratch("xT", [sh.B, P, sh.KD, sh.N])
    scratch("part", [sh.T, sh.D])
    scratch("table", [slots, 1], I32)
    scratch("y", [slots, sh.D])
    scratch("qkT", [sh.B, 3, sh.KD, P, 2, sh.N])
    with ExitStack() as ctx:
        def sb(name, shape, dt=F32):
            return ctx.enter_context(nc.sbuf_tensor(name, shape, dt))

        keep = dict(
            ident=sb("ident", [P, P]),
            slot=sb("slot", [P, 2, sh.NT], I32),
            place=sb("place", [P, 2, sh.NT], I32),
            token=sb("token", [P, sh.NT], I32),
            weight=sb("weight", [P, 2, sh.NT]),
            experts=sb("experts", [1, sh.SLOT_TILES // 2 + sh.DOWN_LAG], I32),
        )
        with ExitStack() as inner:
            keep["xT"] = inner.enter_context(nc.sbuf_tensor("xT_all", [P, sh.KD, sh.T], F32))
            phase_route(nc, sh, dram, keep)
            if phases >= 2:
                phase_shared(nc, sh, dram, keep)
        keep["qkv_part"] = [sb(f"qkv_part{x}", [P, sh.KD, 3 * sh.D], F32R) for x in range(2)]
        keep["proj_part"] = [sb(f"proj_part{x}", [P, sh.KD, sh.D], F32R) for x in range(2)]
        if phases >= 3:
            phase_experts(nc, sh, dram, keep)
        if phases >= 4:
            phase_attention(nc, sh, dram, keep)


def kernel(L0_attn_x, L0_attn_qkv_w, L0_attn_proj_w, L0_attn_proj_b, L0_ffn_Wr, L0_ffn_Wg, L0_ffn_Wu, L0_ffn_Wd,
           L0_ffn_Sg, L0_ffn_Su, L0_ffn_Sd):
    import numpy as np
    import concourse.bacc as bacc
    from concourse.bass_utils import run_bass_kernel_spmd

    arrays = dict(x=L0_attn_x, qkv_wT=np.asarray(L0_attn_qkv_w).T, proj_wT=np.asarray(L0_attn_proj_w).T,
                  proj_b=np.asarray(L0_attn_proj_b).reshape(1, -1), Wr=L0_ffn_Wr, Wg=L0_ffn_Wg, Wu=L0_ffn_Wu,
                  Wd=L0_ffn_Wd, Sg=L0_ffn_Sg, Su=L0_ffn_Su, Sd=L0_ffn_Sd)
    arrays = {f"in_{n}": np.ascontiguousarray(a) for n, a in arrays.items()}
    nc = bacc.Bacc("TRN2", target_bir_lowering=False, num_devices=1)
    args = [nc.dram_tensor(n, a.shape, mybir.dt.from_np(a.dtype), kind="ExternalInput").ap()
            for n, a in arrays.items()]
    args.append(nc.dram_tensor("out", arrays["in_x"].shape, F32, kind="ExternalOutput").ap())
    build(nc, *args)
    return run_bass_kernel_spmd(nc, [arrays], core_ids=[0]).results[0]["out"]
```
